# Optimizing a Trainium2 kernel written in Bass

```python
import numpy as np
import jax
import jax.numpy as jnp

def _softmax(x, axis=-1):
    return jax.nn.softmax(x, axis=axis)

def _gelu(x):
    return jax.nn.gelu(x, approximate=True)

def _silu(x):
    return jax.nn.silu(x)

def _sigmoid(x):
    return jax.nn.sigmoid(x)

def _layernorm(x, axis=-1, eps=1e-05):
    m = jnp.mean(x, axis=axis, keepdims=True)
    v = jnp.var(x, axis=axis, keepdims=True)
    return (x - m) / jnp.sqrt(v + eps)

def _scatter_add(tgt, idx, src, axis=0):
    return tgt.at[idx].add(src)

def _segment_sum(src, seg, n):
    return jax.ops.segment_sum(src, seg, n)
kernel_name = 'mk_sandwich_d1_jaxref_r8_d90a60'

def setup_inputs(seed: int=0):
    np.random.seed(seed)
    _w = jnp.asarray

    def _L0_attn_setup():
        import jax, jax.numpy as jnp
        import numpy as np
        B, S, D = (2, 256, 128)
        H, P = (16, 64)
        NUM_OUT = 128
        key = jax.random.key(seed)
        ks = jax.random.split(key, 9)
        sc = 0.05
        return {'x': jax.random.normal(ks[0], (B, S, D), jnp.float32), 'q_w': jax.random.normal(ks[1], (H, P, D), jnp.float32) * sc, 'q_b': jax.random.normal(ks[2], (H, 1, P), jnp.float32) * sc, 'k_w': jax.random.normal(ks[3], (H, P, D), jnp.float32) * sc, 'k_b': jax.random.normal(ks[4], (H, 1, P), jnp.float32) * sc, 'v_w': jax.random.normal(ks[5], (H, P, D), jnp.float32) * sc, 'v_b': jax.random.normal(ks[6], (H, 1, P), jnp.float32) * sc, 'l_w': jax.random.normal(ks[7], (NUM_OUT, P * H), jnp.float32) * sc, 'l_b': jax.random.normal(ks[8], (1, NUM_OUT), jnp.float32) * sc}
    _L0_attn_in = _L0_attn_setup()

    def _L0_ffn_setup():
        import jax, jax.numpy as jnp
        import numpy as np
        B, S, D, FF, E, L = (8, 256, 128, 512, 16, 4)

        def _unipool_layer(xt, router, W1, W2):
            logits = xt @ router
            probs = jax.nn.softmax(logits, axis=-1)
            w = jnp.max(probs, axis=-1)
            idx = jnp.argmax(probs, axis=-1)

            def body(acc, params):
                w1, w2, i = params
                h = jax.nn.silu(xt @ w1) @ w2
                sel = jnp.where(idx == i, w, 0.0)
                return (acc + sel[:, None] * h, None)
            out, _ = jax.lax.scan(body, jnp.zeros_like(xt), (W1, W2, jnp.arange(W1.shape[0])))
            return out
        key = jax.random.key(seed)
        k0, k1, k2, k3 = jax.random.split(key, 4)
        x = jax.random.normal(k0, (B, S, D), dtype=jnp.float32)
        routers = jax.random.normal(k1, (L, D, E), dtype=jnp.float32) * 0.02
        W1 = jax.random.normal(k2, (E, D, FF), dtype=jnp.float32) * 0.02
        W2 = jax.random.normal(k3, (E, FF, D), dtype=jnp.float32) * 0.02
        return {'x': x, 'routers': routers, 'W1': W1, 'W2': W2}
    _L0_ffn_in = _L0_ffn_setup()
    _d = {'L0_attn_x': _L0_attn_in['x'], 'L0_attn_q_w': _L0_attn_in['q_w'], 'L0_attn_q_b': _L0_attn_in['q_b'], 'L0_attn_k_w': _L0_attn_in['k_w'], 'L0_attn_k_b': _L0_attn_in['k_b'], 'L0_attn_v_w': _L0_attn_in['v_w'], 'L0_attn_v_b': _L0_attn_in['v_b'], 'L0_attn_l_w': _L0_attn_in['l_w'], 'L0_attn_l_b': _L0_attn_in['l_b'], 'L0_ffn_routers': _L0_ffn_in['routers'], 'L0_ffn_W1': _L0_ffn_in['W1'], 'L0_ffn_W2': _L0_ffn_in['W2']}
    _x0 = _d['L0_attn_x']
    _d['L0_attn_x'] = jax.random.normal(jax.random.fold_in(jax.random.key(seed), 1), (4, 512, 128), dtype=_x0.dtype)
    del _x0
    return _d

def reference(L0_attn_x, L0_attn_q_w, L0_attn_q_b, L0_attn_k_w, L0_attn_k_b, L0_attn_v_w, L0_attn_v_b, L0_attn_l_w, L0_attn_l_b, L0_ffn_routers, L0_ffn_W1, L0_ffn_W2):

    def _L0_attn_ref(x, q_w, q_b, k_w, k_b, v_w, v_b, l_w, l_b):
        import jax, jax.numpy as jnp
        import numpy as np
        B, S, D = (2, 256, 128)
        H, P = (16, 64)
        NUM_OUT = 128
        q = jnp.einsum('bsd,hpd->bhsp', x, q_w) + q_b
        k = jnp.einsum('bsd,hpd->bhsp', x, k_w) + k_b
        v = jnp.einsum('bsd,hpd->bhsp', x, v_w) + v_b
        scores = jnp.einsum('bhqp,bhkp->bhqk', q, k) / jnp.sqrt(jnp.float32(P))
        attn = jax.nn.softmax(scores, axis=2)
        ctx = jnp.einsum('bhqk,bhkp->bqhp', attn, v)
        concat = ctx.reshape(ctx.shape[0], ctx.shape[1], H * P)
        out = concat @ l_w.T + l_b
        return out

    def _L0_ffn_ref(x, routers, W1, W2):
        import jax, jax.numpy as jnp
        import numpy as np
        B, S, D, FF, E, L = (8, 256, 128, 512, 16, 4)

        def _unipool_layer(xt, router, W1, W2):
            logits = xt @ router
            probs = jax.nn.softmax(logits, axis=-1)
            w = jnp.max(probs, axis=-1)
            idx = jnp.argmax(probs, axis=-1)

            def body(acc, params):
                w1, w2, i = params
                h = jax.nn.silu(xt @ w1) @ w2
                sel = jnp.where(idx == i, w, 0.0)
                return (acc + sel[:, None] * h, None)
            out, _ = jax.lax.scan(body, jnp.zeros_like(xt), (W1, W2, jnp.arange(W1.shape[0])))
            return out
        b, s, d = x.shape
        xt = x.reshape(-1, d)

        def step(carry, router):
            return (_unipool_layer(carry, router, W1, W2), None)
        xt, _ = jax.lax.scan(step, xt, routers)
        return xt.reshape(b, s, d)
    x = L0_attn_x
    x = x + _layernorm(_L0_attn_ref(_layernorm(x, axis=-1), L0_attn_q_w, L0_attn_q_b, L0_attn_k_w, L0_attn_k_b, L0_attn_v_w, L0_attn_v_b, L0_attn_l_w, L0_attn_l_b), axis=-1)
    x = x + _layernorm(_L0_ffn_ref(_layernorm(x, axis=-1), L0_ffn_routers, L0_ffn_W1, L0_ffn_W2), axis=-1)
    return x

_drawn_inputs = setup_inputs


def setup_inputs(seed=0):
    import zlib

    import numpy as np

    out = dict(_drawn_inputs(seed))
    spreads = {}
    factors = {'L0_attn_q_b': 8.0,
     'L0_attn_k_b': 3.369,
     'L0_ffn_routers': 8.0,
     'L0_ffn_W1': 8.0,
     'L0_ffn_W2': 8.0}
    for name, (base, spread) in spreads.items():
        noise = np.random.default_rng([zlib.crc32(name.encode()), seed]).standard_normal(out[name].shape)
        drawn = base * np.exp(spread * noise) if base else spread * noise
        out[name] = jnp.asarray(drawn.astype(out[name].dtype))
    for name, factor in factors.items():
        out[name] = (out[name] * factor).astype(out[name].dtype)
    return out
```

```python
from contextlib import ExitStack

import concourse.bass as bass
from concourse import mybir

F32 = mybir.dt.float32
F16 = mybir.dt.float16
BF16 = mybir.dt.bfloat16
I32 = mybir.dt.int32
ALU = mybir.AluOpType
ACT = mybir.ActivationFunctionType
AX_X = mybir.AxisListType.X

P = 128
LN_EPS = 1e-5
W_SCALE = 64.0
ROUND = 1.5 * 2.0 ** 23
ROW = P + 4
INVALID = 100.0


def sandwich_kernel(nc, x_in, q_w, q_b, k_w, k_b, v_w, v_b, l_w, l_b, routers, W1, W2, out):
    B, S, D = x_in.shape
    H, DH, _ = q_w.shape
    L, _, E = routers.shape
    FF = W1.shape[2]
    NT = B * S // P
    TPB = S // P
    HD = H * DH
    NPAIR = H // 2
    NP = B * NPAIR
    FC = FF // P
    NS = NT + E
    SG = 4
    assert D == P and DH == 64 and S == 512 and NS * E == 512 and FF == 512

    x_rows = x_in.rearrange("b (t p) d -> p (b t) d", p=P)
    out_rows = out.rearrange("b (t p) d -> p (b t) d", p=P)
    rows = nc.dram_tensor("rows", [NS * P, ROW], F32, kind="Internal").ap()
    ffn_out = nc.dram_tensor("ffn_out", [NT * P, D], F32, kind="Internal").ap()

    with ExitStack() as ctx:
        def sem(name):
            return ctx.enter_context(nc.semaphore(name))

        def sb(name, shape, dt=F32, of=ctx):
            return of.enter_context(nc.sbuf_tensor(name, shape, dt))

        ident = sb("ident", [P, P])
        eps = sb("eps", [P, 1])
        tok_mem = sb("tok_mem", [P, NT * (D + ROW)])
        x_sb = tok_mem[:, 0:NT * D].rearrange("p (t d) -> p t d", d=D)
        xn = tok_mem[:, NT * D:].rearrange("p (t d) -> p t d", d=ROW)
        stats = sb("stats", [P, NT, 6])
        meanvar = sb("meanvar", [P, NT, 2])
        std = sb("std", [P, NT])
        rstd = sb("rstd", [P, NT])
        w1_sb = sb("w1_sb", [P, E * FF])
        w2_sb = sb("w2_sb", [P, E * FC * D])
        router_sb = sb("router_sb", [P, L * E])
        lower_less = sb("lower_less", [P, P], BF16)
        ones = sb("ones", [P, P], BF16)
        iota_b = sb("iota_b", [P, P])
        iota_a = sb("iota_a", [P, NS])
        source1 = sb("source1", [P, NS])
        one_row = sb("one_row", [P, E])
        half = sb("half", [P, NS])

        att = ctx.enter_context(ExitStack())
        xT_hi = sb("xT_hi", [P, NT * P], F16, att)
        xT_lo = sb("xT_lo", [P, NT * P], F16, att)
        wT_hi = sb("wT_hi", [P, 3, HD], F16, att)
        wT_lo = sb("wT_lo", [P, 3, HD], F16, att)
        lwT = sb("lwT", [P, NPAIR, D], F32, att)
        brow = sb("brow", [2 * NPAIR + 1, P], F32, att)
        bcol = sb("bcol", [P, 2 * NPAIR + 1], F32, att)
        vb_all = sb("vb_all", [P, HD], F32, att)
        q_pair = sb("q_pair", [P, 2, 2, S], F16, att)
        k_pair = sb("k_pair", [P, 2, 2, S], F16, att)
        q_stack = sb("q_stack", [P, 2, 2, S], F16, att)
        k_stack = sb("k_stack", [P, 2, 2, 2, S], F16, att)
        v_sb = sb("v_sb", [P, 2, TPB, P], F32, att)
        vp = sb("vp", [P, TPB, P], F32, att)
        e_sb = tok_mem[:, 0:TPB * 2 * S].rearrange("p (t h s) -> p t h s", t=TPB, h=2)
        ctxT = sb("ctxT", [P, NPAIR, B * S], F32, att)
        w_raw = ctxT[:, 0:2, :].rearrange("p a (b j c) -> p (a b) j c", b=2, j=NPAIR)
        mx = sb("mx", [P, TPB, 2], F32, att)
        nmx = sb("nmx", [P, TPB, 2], F32, att)
        minus_sc = sb("minus_sc", [P, 1], F32, att)
        esum = sb("esum", [P, TPB, 2], F32, att)
        rsum = sb("rsum", [P, TPB, 2], F32, att)
        oT = sb("oT", [P, 2, S], F32, att)
        att_n = xn
        att.close()

        keep = sb("keep", [P, E, NS])
        expert_em = sb("expert_em", [P, E, NS])
        expert_jm = sb("expert_jm", [P, NS, E])
        xg = sb("xg", [P, NS, ROW])
        on_b = sb("on_b", [P, NS, P])
        place = sb("place", [P, NS, 2, NS])
        on_a = sb("on_a", [P, NS, NS])
        rel = sb("rel", [P, NS, E])
        cand = sb("cand", [P, NS, E])
        ex = sb("ex", [P, NS, E])
        chosen = sb("chosen", [P, E, NS], BF16)
        incl = sb("incl", [P, E, NS])
        addr = sb("addr", [P, E, NS])
        under = sb("under", [P, NS, E])
        lmax = sb("lmax", [P, NS])
        zsum = sb("zsum", [P, NS])
        weight = sb("weight", [P, NS])
        expert = sb("expert", [P, NS])
        empty = sb("empty", [P, NS])
        pos = sb("pos", [P, NS])
        pos_a = sb("pos_a", [P, NS])
        pos_b = sb("pos_b", [P, NS])
        tiles_e = sb("tiles_e", [P, E])
        cum_e = sb("cum_e", [P, E])
        first_e = sb("first_e", [P, E])
        eid = sb("eid", [P, NS])
        w_off = sb("w_off", [P, NS], I32)
        src_i = sb("src_i", [P, NS], I32)
        w_found = sb("w_found", [P, NS])
        w_slot = sb("w_slot", [P, NS])
        xT = sb("xT", [P, 2, P])
        th = sb("th", [P, 2, FF])
        act_h = sb("act_h", [P, 2, FF])
        hT = sb("hT", [P, 2, FC, P])
        y = sb("y", [P, NS, ROW])
        yT = sb("yT", [P, 2, P])
        tok_i = sb("tok_i", [P, NS], I32)
        rowsT = sb("rowsT", [P, 2, S])
        got = sb("got", [P, NT, D])

        ps = [ctx.enter_context(nc.psum_tensor(f"ps{i}", [P, 512], F32)) for i in range(8)]
        ps_ctx, ps_q, ps_k, ps_v = ps[4:8]

        x_loaded = [sem(f"x_loaded{b}") for b in range(B)]
        b_loaded, w_loaded, vb_loaded, ffn_loaded = sem("b_loaded"), sem("w_loaded"), sem("vb_loaded"), sem("ffn_loaded")
        consts = sem("consts")
        ln_stat, ln_var, ln_std, ln_rstd, ln_out = sem("ln_stat"), sem("ln_var"), sem("ln_std"), sem("ln_rstd"), sem("ln_out")
        prep_T, prep_hi, prep_done = sem("prep_T"), sem("prep_hi"), sem("prep_done")
        q_ready, k_ready, v_ready = sem("q_ready"), sem("k_ready"), sem("v_ready")
        q_hi, k_hi, q_lo, k_lo = sem("q_hi"), sem("k_hi"), sem("q_lo"), sem("k_lo")
        v_out = sem("v_out")
        q_stacked, k_stacked = [sem("q_stacked0"), sem("q_stacked1")], [sem("k_stacked0"), sem("k_stacked1")]
        scores_ready, max_done, nmax_done, exp_done = sem("scores_ready"), sem("max_done"), sem("nmax_done"), sem("exp_done")
        rsum_done, vp_done, ctx_step, ctx_copied = sem("rsum_done"), sem("vp_done"), sem("ctx_step"), sem("ctx_copied")
        proj_ready, proj_copied, projT_ready = sem("proj_ready"), sem("proj_copied"), sem("projT_ready")
        x1_done = sem("x1_done")
        xn_T, xn_copied, rows_written = sem("xn_T"), sem("xn_copied"), sem("rows_written")
        tables, pl_clear, numbered = sem("tables"), sem("pl_clear"), sem("numbered")
        logits_ready, rel_ready, exp_ready = sem("logits_ready"), sem("rel_ready"), sem("exp_ready")
        chosen_ready, counts_ready = sem("chosen_ready"), sem("counts_ready")
        on_b_ready, inv_ready, w_off_ready, src_ready = sem("on_b_ready"), sem("inv_ready"), sem("w_off_ready"), sem("src_ready")
        w_slot_ready = sem("w_slot_ready")
        route = sem("route")
        gathered = [sem(f"gathered{k}") for k in range(NS)]
        xT_in, xT_out, h_in, th_done, h_done = sem("xT_in"), sem("xT_out"), sem("h_in"), sem("th_done"), sem("h_done")
        hT_in, hT_out, y_in, y_done = sem("hT_in"), sem("hT_out"), sem("y_in"), sem("y_done")
        yT_in, yT_out, logit_mm = sem("yT_in"), sem("yT_out"), sem("logit_mm")
        y_written = sem("y_written")
        scattered = sem("scattered")
        got_loaded = [sem(f"got_loaded{b}") for b in range(B)]
        fin_ready, stored = sem("fin_ready"), sem("stored")
        block = ctx.enter_context(nc.Block())

        PL = ps[3]
        ROUTE_STEPS = 24
        SC = float(DH) ** -0.5 / (W_SCALE * W_SCALE)
        PREP = [("w", m, g) for m in range(4) for g in range(2)] + [("x", b, 0) for b in range(B)]
        NPREP = len(PREP)
        NLN = 3

        @block.sync
        def _(sp):
            for b in range(B):
                sp.dma_start(x_sb[:, b * TPB:(b + 1) * TPB, :], x_rows[:, b * TPB:(b + 1) * TPB, :]).then_inc(x_loaded[b], 16)

            def stack_k(u):
                for hd in range(2):
                    for half in range(2):
                        sp.dma_start(k_stack[64 * half:64 * half + 64, u, hd, :, :],
                                     k_pair[64 * hd:64 * hd + 64, u, :, :]).then_inc(k_stacked[u], 16)

            def stack_q(u):
                for half, hd, hl in ((0, 0, 0), (1, 0, 1), (1, 1, 0), (0, 1, 1)):
                    sp.dma_start(q_stack[64 * half:64 * half + 64, u, hd, :],
                                 q_pair[64 * hd:64 * hd + 64, u, hl, :]).then_inc(q_stacked[u], 16)

            for i in range(2):
                sp.wait_ge(k_lo, i + 1)
                stack_k(i)
                sp.wait_ge(q_lo, i + 1)
                stack_q(i)
            with sp.Fori(1, NP // 2) as g:
                scored = [sp.to_reg(16 * g - 8), sp.to_reg(16 * g)]
                written = [sp.to_reg(2 * g + 1), sp.to_reg(2 * g + 2)]
                for u in range(2):
                    sp.wait_ge(scores_ready, scored[u])
                    sp.wait_ge(k_lo, written[u])
                    stack_k(u)
                    sp.wait_ge(q_lo, written[u])
                    stack_q(u)
            sp.wait_ge(ctx_step, 4 * NP)
            for b in range(B):
                sp.dma_start(x_sb[:, b * TPB:(b + 1) * TPB, :], x_rows[:, b * TPB:(b + 1) * TPB, :]).then_inc(x_loaded[b], 16)
            sp.wait_ge(numbered, 1)
            for b in range(B):
                sp.wait_ge(ln_out, B + 2 * b + 2)
                sp.dma_start(rows[b * S:(b + 1) * S, :].rearrange("(t p) d -> p t d", p=P),
                             xn[:, b * TPB:(b + 1) * TPB, :]).then_inc(rows_written, 16)
            sp.dma_start(rows[NT * P:NS * P, :].rearrange("(t p) d -> p t d", p=P), xn[:, 0:NS - NT, :]).then_inc(rows_written, 16)

            with sp.Fori(0, L - 1) as l:
                counts = [sp.to_reg(l * NS + t + SG) for t in range(0, NS, SG)]
                sp.wait_ge(xT_in, sp.to_reg(l * NS + NS))
                for n, t in enumerate(range(0, NS, SG)):
                    sp.wait_ge(y_done, counts[n])
                    sp.dma_start(rows[t * P:(t + SG) * P, :].rearrange("(t p) d -> p t d", p=P),
                                 y[:, t:t + SG, :]).then_inc(y_written, 16)

            sp.wait_ge(scattered, 16 * NS)
            for b in range(B):
                sp.dma_start(got[:, b * TPB:(b + 1) * TPB, :],
                             ffn_out[b * S:(b + 1) * S, :].rearrange("(t p) d -> p t d", p=P)).then_inc(got_loaded[b], 16)
            for b in range(B):
                sp.wait_ge(fin_ready, b + 1)
                sp.dma_start(out_rows[:, b * TPB:(b + 1) * TPB, :], got[:, b * TPB:(b + 1) * TPB, :]).then_inc(stored, 16)
            sp.wait_ge(stored, 16 * B)

        @block.gpsimd
        def _(pool):
            nc.gpsimd.memset(ident[:, :], 0.0).then_inc(consts, 1)
            nc.gpsimd.memset(eps[:, :], LN_EPS).then_inc(consts, 1)
            pool.wait_ge(consts, 2)
            nc.gpsimd.affine_select(out=ident[:, :], in_=ident[:, :], compare_op=ALU.not_equal, fill=1.0,
                                    base=0, pattern=[[-1, P]], channel_multiplier=1).then_inc(consts, 1)
            nc.gpsimd.memset(minus_sc[:, :], -SC).then_inc(consts, 1)
            g = dict(allow_small_or_imprecise_dtypes=True)
            nc.gpsimd.iota(iota_b[:, :], [[1, P]], base=0, channel_multiplier=0, **g).then_inc(consts, 1)
            nc.gpsimd.iota(iota_a[:, :], [[1, NS]], base=0, channel_multiplier=0, **g).then_inc(consts, 1)
            nc.gpsimd.iota(source1[:, :], [[P, NS]], base=1, channel_multiplier=1, **g).then_inc(consts, 1)
            nc.gpsimd.memset(one_row[:, :], 1.0).then_inc(consts, 1)
            nc.gpsimd.memset(half[:, :], 0.5).then_inc(consts, 1)
            nc.gpsimd.memset(ones[:, :], 1.0).then_inc(consts, 1)
            nc.gpsimd.memset(lower_less[:, :], -1.0).then_inc(consts, 1)
            pool.wait_ge(consts, 11)
            nc.gpsimd.affine_select(out=lower_less[:, :], in_=lower_less[:, :], compare_op=ALU.is_ge, fill=0.0,
                                    base=0, pattern=[[-1, P]], channel_multiplier=1).then_inc(consts, 1)
            pool.dma_start(router_sb[:, :].rearrange("p (l e) -> p l e", l=L),
                           routers.rearrange("l d e -> d l e")).then_inc(ffn_loaded, 16)
            pool.dma_start(w1_sb[:, :].rearrange("p (e f) -> p e f", e=E),
                           W1.rearrange("e d f -> d e f")).then_inc(ffn_loaded, 16)
            pool.dma_start(w2_sb[:, :].rearrange("p (e c d) -> p e c d", e=E, c=FC),
                           W2.rearrange("e (c p) d -> p e c d", p=P)).then_inc(ffn_loaded, 16)
            with pool.Fori(0, NP) as i:
                for n in range(2 * TPB):
                    pool.wait_ge(max_done, 8 * i + (n + 1))
                    nc.gpsimd.tensor_tensor(nmx[:, n // 2, n % 2:n % 2 + 1], mx[:, n // 2, n % 2:n % 2 + 1],
                                            minus_sc[:, :], ALU.mult).then_inc(nmax_done, 1)

            pool.wait_ge(ctx_step, 4 * NP)
            nc.gpsimd.iota(xn[:, :, D:ROW], [[P, NT], [0, ROW - D]], base=0, channel_multiplier=1,
                           allow_small_or_imprecise_dtypes=True).then_inc(numbered, 1)
            pool.wait_ge(projT_ready, B)
            f = dict(allow_small_or_imprecise_dtypes=True, channel_multiplier=0)
            nc.gpsimd.iota(expert_jm[:, :, :], [[0, NS], [1, E]], base=-E, **f).then_inc(tables, 1)
            nc.gpsimd.iota(expert_em[:, :, :], [[1, E], [0, NS]], base=-E, **f).then_inc(tables, 1)
            nc.gpsimd.memset(keep[:, :, 1:NS], 1.0).then_inc(tables, 1)
            nc.gpsimd.memset(keep[:, :, 0:1], 0.0).then_inc(tables, 1)
            nc.gpsimd.memset(empty[:, 0:NT], 0.0).then_inc(tables, 1)
            nc.gpsimd.memset(empty[:, NT:NS], INVALID).then_inc(tables, 1)

            def gather(l):
                if isinstance(l, int) and l == 0:
                    pool.wait_ge(rows_written, 16 * (B + 1))
                else:
                    pool.wait_ge(y_written, 16 * (NS // SG) * l)
                pool.wait_ge(src_ready, l + 1)
                nc.gpsimd.tensor_tensor(w_slot[:, :], w_found[:, :], half[:, :], ALU.mult).then_inc(w_slot_ready, 1)
                for t in range(NS):
                    pool.indirect_dma_start(xg[:, t, :], None, rows, bass.IndirectOffsetOnAxis(ap=src_i[:, t:t + 1], axis=0)
                                            ).then_inc(gathered[t], 16)
                    if isinstance(l, int) and l == L - 1 and t >= 8:
                        scatter(t - 8)

            def scatter(t):
                pool.wait_ge(y_done, NS * (L - 1) + t + 1)
                pool.indirect_dma_start(ffn_out, bass.IndirectOffsetOnAxis(ap=tok_i[:, t:t + 1], axis=0), y[:, t, 0:D], None,
                                        bounds_check=NT * P - 1, oob_is_err=False).then_inc(scattered, 16)

            gather(0)
            with pool.Fori(1, L - 1) as l:
                gather(l)
            gather(L - 1)
            for t in range(NS - 8, NS):
                scatter(t)

        @block.tensor
        def _(pe):
            pe.wait_ge(consts, 3)
            pe.wait_ge(b_loaded, 48)
            nb = 2 * NPAIR + 1
            nc.tensor.transpose(ps_v[:, 0:nb], brow[:, :], ident[0:nb, 0:nb]).then_inc(prep_T, 1)
            pe.wait_ge(w_loaded, 16 * 4)
            for n, (kind, m, g) in enumerate(PREP):
                if n >= 4:
                    pe.wait_ge(prep_done, n - 3 + 1)
                if kind == "x":
                    pe.wait_ge(ln_out, m + 1)
                for c in range(4):
                    src_ = w_raw[:, m, 4 * g + c, :] if kind == "w" else xn[:, TPB * m + c, 0:D]
                    last = nc.tensor.transpose(ps[n % 4][:, c * P:(c + 1) * P], src_, ident[:, :])
                last.then_inc(prep_T, 1)

            PASSES = [(wT_hi, xT_hi), (wT_lo, xT_hi), (wT_hi, xT_lo)]

            def project_qk(dst, m, tok, pair):
                for n, (w, x) in enumerate(PASSES):
                    last = nc.tensor.matmul(dst[:, :], w[:, m, bass.ds(pair * P, P)], x[:, bass.ds(tok, S)],
                                            start=(n == 0), stop=(n == 2))
                return last

            def project_v(tok, pair):
                for t in range(TPB):
                    for n, (w, x) in enumerate(PASSES):
                        last = nc.tensor.matmul(ps_v[:, t * P:(t + 1) * P], x[:, bass.ds(tok + t * P, P)],
                                                w[:, 2, bass.ds(pair * P, P)], start=(n == 0), stop=(n == 2))
                return last

            def scores(i, u, kt, first):
                if kt == 0:
                    pe.wait_ge(q_stacked[u], 32 * i + (64 - 32 * u))
                    pe.wait_ge(k_stacked[u], 32 * i + (64 - 32 * u))
                for hd in range(2):
                    n = 2 * kt + hd
                    if not (first and n < 4):
                        pe.wait_ge(exp_done, 8 * i + (n - 3))
                    for hl in range(2):
                        last = nc.tensor.matmul(ps[n % 4][:, :], k_stack[:, u, hd, hl, kt * P:(kt + 1) * P],
                                                q_stack[:, u, hd, :], start=(hl == 0), stop=(hl == 1))
                    last.then_inc(scores_ready, 1)

            def context(i, kt, first=False):
                if kt == 0 and not first:
                    pe.wait_ge(ctx_copied, i)
                pe.wait_ge(vp_done, 4 * i + (kt + 1))
                for hd in range(2):
                    last = nc.tensor.matmul(ps_ctx[64 * hd:64 * hd + 64, :], vp[:, kt, 64 * hd:64 * hd + 64],
                                            e_sb[:, kt, hd, :], start=(kt == 0), stop=(kt == TPB - 1))
                last.then_inc(ctx_step, 1)

            def pair_step(i, u, first=False, second=False, ahead=2):
                for kt in range(TPB):
                    scores(i, u, kt, first)
                    if ahead >= 1 and kt == 2:
                        pe.wait_ge(v_out, i + 1)
                        project_v(((i + 1) // NPAIR) * S, (i + 1) % NPAIR).then_inc(v_ready, 1)
                    if ahead >= 2 and kt == 0:
                        pe.wait_ge(k_lo, i + 2)
                        project_qk(ps_k, 1, ((i + 2) // NPAIR) * S, (i + 2) % NPAIR).then_inc(k_ready, 1)
                    if ahead >= 2 and kt == 1:
                        pe.wait_ge(q_lo, i + 2)
                        project_qk(ps_q, 0, ((i + 2) // NPAIR) * S, (i + 2) % NPAIR).then_inc(q_ready, 1)
                    if not first:
                        context(i - 1, kt, first=second)

            pe.wait_ge(prep_done, NPREP + 1)
            project_qk(ps_k, 1, 0, 0).then_inc(k_ready, 1)
            project_qk(ps_q, 0, 0, 0).then_inc(q_ready, 1)
            project_v(0, 0).then_inc(v_ready, 1)
            pe.wait_ge(k_lo, 1)
            project_qk(ps_k, 1, 0, 1).then_inc(k_ready, 1)
            pe.wait_ge(q_lo, 1)
            project_qk(ps_q, 0, 0, 1).then_inc(q_ready, 1)
            pair_step(0, 0, first=True)
            pair_step(1, 1, second=True)
            with pe.Fori(1, NP // 2 - 1) as g:
                for u in range(2):
                    pair_step(2 * g + u, u)
            pair_step(NP - 2, 0, ahead=1)
            pair_step(NP - 1, 1, ahead=0)
            for kt in range(TPB):
                context(NP - 1, kt)

            def back(b):
                pe.wait_ge(proj_copied, b + 1)
                for c in range(TPB):
                    last = nc.tensor.transpose(ps[4 + b][:, c * P:(c + 1) * P], oT[:, b % 2, c * P:(c + 1) * P], ident[:, :])
                last.then_inc(projT_ready, 1)

            pe.wait_ge(ctx_copied, NP)
            for b in range(B):
                if b >= 2:
                    pe.wait_ge(proj_copied, b - 1)
                for j in range(NPAIR):
                    last = nc.tensor.matmul(ps[b % 2][:, :], lwT[:, j, :], ctxT[:, j, b * S:(b + 1) * S],
                                            start=(j == 0), stop=(j == NPAIR - 1))
                last.then_inc(proj_ready, 1)
                if b >= 1:
                    back(b - 1)
            back(B - 1)

            pe.wait_ge(ffn_loaded, 48)
            pe.wait_ge(pl_clear, 1)
            for b in range(B):
                pe.wait_ge(ln_out, B + 2 * b + 2)
                for c in range(TPB):
                    last = nc.tensor.transpose(ps[2][:, c * P:(c + 1) * P], xn[:, b * TPB + c, 0:D], ident[:, :])
                last.then_inc(xn_T, 1)
                pe.wait_ge(xn_copied, b + 1)
                for c in range(TPB):
                    j = b * TPB + c
                    last = nc.tensor.matmul(PL[:, j * E:(j + 1) * E], rowsT[:, b % 2, c * P:(c + 1) * P],
                                            router_sb[:, 0:E], start=True, stop=True)
            last.then_inc(logits_ready, 1)

            OG = 8
            offs = [pe.alloc_register(f"w_off{t}") for t in range(2 * OG)]

            def experts(l, final=False):
                base = l * NS
                pe.wait_ge(chosen_ready, l + 1)
                ch = chosen[:, :, :].rearrange("p e j -> p (e j)")
                nc.tensor.matmul(ps[4][:, :], lower_less[:, :], ch, start=True, stop=True).then_inc(counts_ready, 1)
                nc.tensor.matmul(ps[5][:, :], ones[:, :], ch, start=True, stop=True).then_inc(counts_ready, 1)
                for j in range(NS):
                    if j == NS - 1:
                        pe.wait_ge(w_off_ready, l + 1)
                    pe.wait_ge(on_b_ready, base + (j + 1))
                    last = nc.tensor.matmul(ps[6][:, 0:2 * NS], on_b[:, j, :], place[:, j, :, :].rearrange("p a b -> p (a b)"),
                                            start=(j == 0), stop=(j == NS - 1))
                last.then_inc(inv_ready, 1)
                off = {}
                lag = 3 if final else 4
                for s in range(NS + lag):
                    if s % OG == 0 and s < NS:
                        half = (s // OG) % 2 * OG
                        pe.load(offs[half:half + OG], w_off[0:1, s:s + OG])
                        for t in range(OG):
                            off[s + t] = pe.snap(offs[half + t], min_val=0, max_val=(E - 1) * FF)
                    if s < NS:
                        pe.wait_ge(gathered[s], 16 * l + 16)
                        if s > 0:
                            pe.wait_ge(xT_out, base + s)
                        nc.tensor.transpose(ps[0][:, 0:P], xg[:, s, 0:D], ident[:, :]).then_inc(xT_in, 1)
                    t = s - 2
                    if 0 <= t < NS:
                        pe.wait_ge(h_done, base + (t + 1))
                        if t >= 2:
                            pe.wait_ge(hT_out, base + (t - 1))
                        for c in range(FC):
                            last = nc.tensor.transpose(ps[6 + t % 2][:, c * P:(c + 1) * P],
                                                       act_h[:, t % 2, c * P:(c + 1) * P], ident[:, :])
                        last.then_inc(hT_in, 1)
                    if s < NS:
                        pe.wait_ge(xT_out, base + (s + 1))
                        if s >= 2:
                            pe.wait_ge(h_done, base + (s - 1))
                        nc.tensor.matmul(ps[4 + s % 2][:, :], xT[:, s % 2, :], w1_sb[:, bass.ds(off[s], FF)],
                                         start=True, stop=True).then_inc(h_in, 1)
                    t = s - 4
                    if not final and 0 <= t < NS:
                        pe.wait_ge(y_done, base + (t + 1))
                        if t > 0:
                            pe.wait_ge(yT_out, base + t)
                        nc.tensor.transpose(ps[1][:, 0:P], y[:, t, 0:D], ident[:, :]).then_inc(yT_in, 1)
                    t = s - 3
                    if 0 <= t < NS:
                        pe.wait_ge(hT_out, base + (t + 1))
                        if t > 0:
                            pe.wait_ge(y_done, base + t)
                        for c in range(FC):
                            last = nc.tensor.matmul(ps[2][:, 0:D], hT[:, t % 2, c, :],
                                                    w2_sb[:, bass.ds(off[t] + c * D, D)], start=(c == 0), stop=(c == FC - 1))
                        last.then_inc(y_in, 1)
                    t = s - 4
                    if not final and 0 <= t < NS:
                        pe.wait_ge(yT_out, base + (t + 1))
                        nc.tensor.matmul(PL[:, t * E:(t + 1) * E], yT[:, t % 2, :],
                                         router_sb[:, bass.ds((l + 1) * E, E)], start=True, stop=True).then_inc(logit_mm, 1)

            with pe.Fori(0, L - 1) as l:
                experts(l)
            experts(L - 1, final=True)

        @block.scalar
        def _(act):
            for m, (dst, bias) in enumerate(((0, q_b), (NPAIR, k_b))):
                act.dma_start(brow[dst:dst + NPAIR, :], bias.rearrange("(j r) o p -> j (r o p)", r=2)).then_inc(b_loaded, 16)
            act.dma_start(brow[2 * NPAIR:2 * NPAIR + 1, :], l_b).then_inc(b_loaded, 16)
            for m, w in enumerate((q_w, k_w, v_w)):
                act.dma_start(w_raw[:, m], w.rearrange("(j r) p d -> (r p) j d", r=2)).then_inc(w_loaded, 16)
            act.dma_start(w_raw[:, 3], l_w.rearrange("o (j p) -> o j p", p=P)).then_inc(w_loaded, 16)
            act.dma_start(vb_all[:, :], v_b.rearrange("h o p -> o (h p)").broadcast_to([P, HD])).then_inc(vb_loaded, 16)

            act.wait_ge(consts, 2)

            def sqrt(k):
                act.wait_ge(ln_var, k + 1)
                if k == 0:
                    sl = slice(0, NT)
                else:
                    b_ = (k - 1) // 2 if k <= 2 * B else k - 2 * B - 1
                    sl = slice(TPB * b_, TPB * b_ + TPB)
                nc.scalar.activation(std[:, sl], meanvar[:, sl, 1], ACT.Sqrt, bias=eps[:, 0:1]).then_inc(ln_std, 1)

            for n, (kind, m, g) in enumerate(PREP):
                if n == 2:
                    sqrt(0)
                if kind == "w" and m == 3:
                    continue
                act.wait_ge(prep_T, n + 2)
                if kind == "w":
                    nc.scalar.activation(wT_hi[:, m, 512 * g:512 * g + 512], ps[n % 4][:, :], ACT.Copy,
                                         scale=W_SCALE).then_inc(prep_hi, 1)
                else:
                    nc.scalar.activation(xT_hi[:, S * m:S * m + S], ps[n % 4][:, :], ACT.Copy).then_inc(prep_hi, 1)

            def high(dst, u, src_, ready, done, stacked, i, col):
                act.wait_ge(ready, i + 1)
                if stacked is not None:
                    act.wait_ge(stacked[u], 32 * i - 32 * u)
                nc.scalar.activation(dst[:, u, 0, :], src_[:, :], ACT.Identity, bias=bcol[:, bass.ds(col, 1)]).then_inc(done, 1)

            def k_high(i, u, pair, first=False):
                high(k_pair, u, ps_k, k_ready, k_hi, None if first else k_stacked, i, pair + NPAIR)

            def q_high(i, u, pair, first=False):
                high(q_pair, u, ps_q, q_ready, q_hi, None if first else q_stacked, i, pair)

            def copy_context(i):
                act.wait_ge(ctx_step, 4 * i + 4)
                flat = ctxT[:, :, :].rearrange("p j t -> p (j t)")
                nc.scalar.activation(flat[:, bass.ds((i % NPAIR) * (B * S) + (i // NPAIR) * S, S)], ps_ctx[:, :],
                                     ACT.Copy).then_inc(ctx_copied, 1)

            def pair_step(i, u, first=False, project=True):
                for kt in range(TPB):
                    if not first:
                        act.wait_ge(ctx_step, 4 * i + (kt - 3))
                    for hd in range(2):
                        act.wait_ge(nmax_done, 8 * i + (2 * kt + hd + 1))
                        nc.scalar.activation(e_sb[:, kt, hd, :], ps[(2 * kt + hd) % 4][:, :], ACT.Exp,
                                             bias=nmx[:, kt, hd:hd + 1], scale=SC,
                                             accum_out=esum[:, kt, hd:hd + 1]).then_inc(exp_done, 1)
                        if not first and kt == TPB - 1 and hd == 0:
                            copy_context(i - 1)
                    if project and kt == 1:
                        k_high(i + 2, u, (i + 2) % NPAIR)
                    if project and kt == 2:
                        q_high(i + 2, u, (i + 2) % NPAIR)
            act.wait_ge(prep_done, 1)
            for i in range(2):
                k_high(i, i, i, first=True)
                q_high(i, i, i, first=True)
            pair_step(0, 0, first=True)
            pair_step(1, 1)
            with act.Fori(1, NP // 2 - 1) as g:
                for u in range(2):
                    pair_step(2 * g + u, u)
            pair_step(NP - 2, 0, project=False)
            pair_step(NP - 1, 1, project=False)
            copy_context(NP - 1)

            def copy_rows(b):
                act.wait_ge(xn_T, b + 1)
                nc.scalar.activation(rowsT[:, b % 2, :], ps[2][:, :], ACT.Copy).then_inc(xn_copied, 1)

            for b in range(B):
                act.wait_ge(proj_ready, b + 1)
                if b >= 2:
                    act.wait_ge(projT_ready, b - 1)
                nc.scalar.activation(oT[:, b % 2, :], ps[b % 2][:, :], ACT.Identity,
                                     bias=bcol[:, 2 * NPAIR:2 * NPAIR + 1]).then_inc(proj_copied, 1)
                if b >= 1:
                    sqrt(2 * b - 1)
                    sqrt(2 * b)
            sqrt(2 * B - 1)
            sqrt(2 * B)
            for b in range(B):
                copy_rows(b)

            def experts(l, final=False):
                base = l * NS
                act.wait_ge(rel_ready, l + 1)
                nc.scalar.activation(ex[:, :, :], rel[:, :, :], ACT.Exp).then_inc(exp_ready, 1)
                for s in range(NS + (0 if final else 4)):
                    if s < NS:
                        act.wait_ge(xT_in, base + (s + 1))
                        if s >= 2:
                            act.wait_ge(h_in, base + (s - 1))
                        nc.scalar.activation(xT[:, s % 2, :], ps[0][:, 0:P], ACT.Copy).then_inc(xT_out, 1)
                        act.wait_ge(h_in, base + (s + 1))
                        if s >= 2:
                            act.wait_ge(h_done, base + (s - 1))
                        nc.scalar.activation(th[:, s % 2, :], ps[4 + s % 2][:, :], ACT.Tanh, scale=0.5).then_inc(th_done, 1)
                    t = s - 4
                    if not final and 0 <= t < NS:
                        act.wait_ge(yT_in, base + (t + 1))
                        if t >= 2:
                            act.wait_ge(logit_mm, base + (t - 1))
                        nc.scalar.activation(yT[:, t % 2, :], ps[1][:, 0:P], ACT.Copy).then_inc(yT_out, 1)

            with act.Fori(0, L - 1) as l:
                experts(l)
            experts(L - 1, final=True)
            for b in range(B):
                sqrt(2 * B + 1 + b)

        @block.vector
        def _(dve):
            def variance(k, rows_of, tiles):
                for t in tiles:
                    last = nc.vector.bn_stats(stats[:, t, :], rows_of(t))
                last.then_inc(ln_stat, 1)
                dve.wait_ge(ln_stat, k + 1)
                for t in tiles:
                    last = nc.vector.bn_aggr(meanvar[:, t, :], stats[:, t, :])
                last.then_inc(ln_var, 1)

            def inverse(k, tiles):
                dve.wait_ge(ln_std, k + 1)
                sl = slice(tiles[0], tiles[-1] + 1)
                nc.vector.reciprocal(rstd[:, sl], std[:, sl]).then_inc(ln_rstd, 1)
                dve.wait_ge(ln_rstd, k + 1)

            for b in range(B):
                dve.wait_ge(x_loaded[b], 16)
                for t in range(TPB * b, TPB * b + TPB):
                    last = nc.vector.bn_stats(stats[:, t, :], x_sb[:, t, :])
            last.then_inc(ln_stat, 1)
            dve.wait_ge(ln_stat, 1)
            for t in range(NT):
                last = nc.vector.bn_aggr(meanvar[:, t, :], stats[:, t, :])
            last.then_inc(ln_var, 1)
            dve.wait_ge(prep_T, 1)
            nc.vector.tensor_scalar(bcol[:, 0:2 * NPAIR], ps_v[:, 0:2 * NPAIR], W_SCALE, None, ALU.mult)
            nc.vector.tensor_copy(bcol[:, 2 * NPAIR:2 * NPAIR + 1], ps_v[:, 2 * NPAIR:2 * NPAIR + 1]).then_inc(prep_done, 1)
            for n, (kind, m, g) in enumerate(PREP):
                if n == 3:
                    inverse(0, range(NT))
                    for b in range(B):
                        for t in range(TPB * b, TPB * b + TPB):
                            last = nc.vector.tensor_scalar(xn[:, t, 0:D], x_sb[:, t, :], meanvar[:, t, 0:1],
                                                           rstd[:, t:t + 1], ALU.subtract, ALU.mult)
                        last.then_inc(ln_out, 1)
                if kind == "w" and m == 3:
                    dve.wait_ge(prep_T, n + 2)
                    nc.vector.tensor_copy(lwT[:, 4 * g:4 * g + 4, :].rearrange("p a b -> p (a b)"),
                                          ps[n % 4][:, :]).then_inc(prep_done, 1)
                    continue
                dve.wait_ge(prep_hi, n + 1 if kind == "w" else n - 1)
                if kind == "w":
                    nc.vector.scalar_tensor_tensor(out=wT_lo[:, m, 512 * g:512 * g + 512], in0=ps[n % 4][:, :],
                                                   scalar=W_SCALE, in1=wT_hi[:, m, 512 * g:512 * g + 512],
                                                   op0=ALU.mult, op1=ALU.subtract).then_inc(prep_done, 1)
                else:
                    nc.vector.tensor_tensor(xT_lo[:, S * m:S * m + S], ps[n % 4][:, :], xT_hi[:, S * m:S * m + S],
                                            ALU.subtract).then_inc(prep_done, 1)

            def low(dst, u, src_, hi, done, col, i):
                dve.wait_ge(hi, i + 1)
                nc.vector.scalar_tensor_tensor(out=dst[:, u, 1, :], in0=src_[:, :], scalar=bcol[:, bass.ds(col, 1)],
                                               in1=dst[:, u, 0, :], op0=ALU.add, op1=ALU.subtract).then_inc(done, 1)

            def values(i, u, pair):
                dve.wait_ge(v_ready, i + 1)
                nc.vector.scalar_tensor_tensor(
                    out=v_sb[:, u, :, :], in0=ps_v[:, :].rearrange("p (t c) -> p t c", t=TPB), scalar=1.0 / W_SCALE,
                    in1=vb_all[:, bass.ds(pair * P, P)].unsqueeze(1).broadcast_to([P, TPB, P]),
                    op0=ALU.mult, op1=ALU.add).then_inc(v_out, 1)

            def scale_values(i, u, kt):
                dve.wait_ge(exp_done, 8 * i + (2 * kt + 2))
                nc.vector.reciprocal(rsum[:, kt, :], esum[:, kt, :]).then_inc(rsum_done, 1)
                dve.wait_ge(rsum_done, 4 * i + (kt + 1))
                nc.vector.tensor_tensor(vp[:, kt, :].rearrange("p (h c) -> p h c", h=2),
                                        v_sb[:, u, kt, :].rearrange("p (h c) -> p h c", h=2),
                                        rsum[:, kt, :].unsqueeze(2).broadcast_to([P, 2, DH]),
                                        ALU.mult).then_inc(vp_done, 1)

            def pair_step(i, u, ahead=2, first=False):
                for kt in range(TPB):
                    for hd in range(2):
                        dve.wait_ge(scores_ready, 8 * i + (2 * kt + hd + 1))
                        nc.vector.tensor_reduce(mx[:, kt, hd:hd + 1], ps[(2 * kt + hd) % 4][:, :], AX_X,
                                                ALU.max).then_inc(max_done, 1)
                    if kt >= 1:
                        scale_values(i, u, kt - 1)
                    elif not first:
                        scale_values(i - 1, 1 - u, TPB - 1)
                    if kt == 0 and not first:
                        values(i, u, i % NPAIR)
                    if ahead >= 2 and kt == 2:
                        low(k_pair, u, ps_k, k_hi, k_lo, (i + 2) % NPAIR + NPAIR, i + 2)
                    if ahead >= 2 and kt == 3:
                        low(q_pair, u, ps_q, q_hi, q_lo, (i + 2) % NPAIR, i + 2)

            low(k_pair, 0, ps_k, k_hi, k_lo, NPAIR, 0)
            low(q_pair, 0, ps_q, q_hi, q_lo, 0, 0)
            dve.wait_ge(vb_loaded, 16)
            values(0, 0, 0)
            low(k_pair, 1, ps_k, k_hi, k_lo, NPAIR + 1, 1)
            low(q_pair, 1, ps_q, q_hi, q_lo, 1, 1)
            pair_step(0, 0, first=True)
            pair_step(1, 1)
            with dve.Fori(1, NP // 2 - 1) as g:
                for u in range(2):
                    pair_step(2 * g + u, u)
            pair_step(NP - 2, 0, ahead=1)
            pair_step(NP - 1, 1, ahead=0)
            scale_values(NP - 1, 1, TPB - 1)

            nc.vector.memset(PL[:, :], 0.0).then_inc(pl_clear, 1)
            for b in range(B):
                tiles = range(TPB * b, TPB * b + TPB)
                k = 1 + 2 * b
                dve.wait_ge(projT_ready, b + 1)
                variance(k, lambda t: ps[4 + b][:, (t % TPB) * P:(t % TPB + 1) * P], tiles)
                inverse(k, tiles)
                for t in tiles:
                    last = nc.vector.tensor_scalar(att_n[:, t, 0:D], ps[4 + b][:, (t % TPB) * P:(t % TPB + 1) * P],
                                                   meanvar[:, t, 0:1], rstd[:, t:t + 1], ALU.subtract, ALU.mult)
                last.then_inc(ln_out, 1)
                dve.wait_ge(ln_out, B + 2 * b + 1)
                sl = slice(TPB * b, TPB * b + TPB)
                dve.wait_ge(x_loaded[b], 32)
                nc.vector.tensor_tensor(x_sb[:, sl, :], x_sb[:, sl, :], att_n[:, sl, 0:D], ALU.add).then_inc(x1_done, 1)
                dve.wait_ge(x1_done, b + 1)
                variance(k + 1, lambda t: x_sb[:, t, :], tiles)
                inverse(k + 1, tiles)
                for t in tiles:
                    last = nc.vector.tensor_scalar(xn[:, t, 0:D], x_sb[:, t, :], meanvar[:, t, 0:1],
                                                   rstd[:, t:t + 1], ALU.subtract, ALU.mult)
                last.then_inc(ln_out, 1)

            count = [0]

            def step(ins, l):
                count[0] += 1
                ins.then_inc(route, 1)
                dve.wait_ge(route, l * ROUTE_STEPS + count[0])

            def send_rows(l):
                count[0] = 0
                V = nc.vector
                pl = PL[:, :].rearrange("p (j e) -> p j e", e=E)
                if isinstance(l, int) and l == 0:
                    dve.wait_ge(logits_ready, 1)
                    dve.wait_ge(tables, 6)
                    dve.wait_ge(consts, 12)
                else:
                    dve.wait_ge(logit_mm, NS * l)
                step(V.tensor_reduce(lmax[:, :], pl, AX_X, ALU.max), l)
                ins = V.tensor_tensor(rel[:, :, :], pl, lmax[:, :].unsqueeze(2).broadcast_to([P, NS, E]), ALU.subtract)
                ins.then_inc(rel_ready, 1)
                dve.wait_ge(rel_ready, l + 1)
                step(V.scalar_tensor_tensor(out=cand[:, :, :], in0=rel[:, :, :], scalar=0.0, in1=expert_jm[:, :, :],
                                            op0=ALU.is_equal, op1=ALU.mult), l)
                step(V.tensor_reduce(expert[:, :], cand[:, :, :], AX_X, ALU.min), l)
                step(V.tensor_tensor(expert[:, :], expert[:, :], empty[:, :], ALU.add), l)
                V.tensor_tensor(chosen[:, :, :], expert_em[:, :, :], expert[:, :].unsqueeze(1).broadcast_to([P, E, NS]),
                                ALU.is_equal).then_inc(chosen_ready, 1)
                dve.wait_ge(exp_ready, l + 1)
                step(V.tensor_reduce(zsum[:, :], ex[:, :, :], AX_X, ALU.add), l)
                step(V.reciprocal(weight[:, :], zsum[:, :]), l)
                dve.wait_ge(counts_ready, 2 * l + 2)
                flat = lambda a: a[:, :, :].rearrange("p e j -> p (e j)")
                step(V.tensor_tensor_scan(flat(incl), flat(keep), ps[5][:, :], 0.0, ALU.mult, ALU.add), l)
                step(V.tensor_scalar(tiles_e[:, :], incl[:, :, NS - 1], (P - 1) / 2.0, 1.0 / P, ALU.add, ALU.mult), l)
                step(V.tensor_scalar(tiles_e[:, :], tiles_e[:, :], ROUND, ROUND, ALU.add, ALU.subtract), l)
                step(V.tensor_tensor_scan(cum_e[:, :], one_row[:, :], tiles_e[:, :], 0.0, ALU.mult, ALU.add), l)
                step(V.tensor_tensor(first_e[:, :], cum_e[:, :], tiles_e[:, :], ALU.subtract), l)
                step(V.scalar_tensor_tensor(out=addr[:, :, :], in0=first_e[:, :].unsqueeze(2).broadcast_to([P, E, NS]),
                                            scalar=float(P), in1=incl[:, :, :], op0=ALU.mult, op1=ALU.add), l)
                step(V.tensor_tensor(flat(addr), ps[4][:, :], flat(addr), ALU.add), l)
                step(V.tensor_tensor(addr[:, :, :], addr[:, :, :], chosen[:, :, :], ALU.mult), l)
                step(V.tensor_reduce(pos[:, :], addr[:, :, :].rearrange("p e j -> p j e"), AX_X, ALU.add), l)
                step(V.scalar_tensor_tensor(out=pos[:, :], in0=empty[:, :], scalar=100.0, in1=pos[:, :],
                                            op0=ALU.mult, op1=ALU.add), l)
                step(V.tensor_scalar(pos_a[:, :], pos[:, :], -(P - 1) / 2.0, 1.0 / P, ALU.add, ALU.mult), l)
                step(V.tensor_scalar(pos_a[:, :], pos_a[:, :], ROUND, ROUND, ALU.add, ALU.subtract), l)
                step(V.scalar_tensor_tensor(out=pos_b[:, :], in0=pos_a[:, :], scalar=-float(P), in1=pos[:, :],
                                            op0=ALU.mult, op1=ALU.add), l)
                step(V.tensor_tensor(under[:, :, :], cum_e[:, :].unsqueeze(1).broadcast_to([P, NS, E]),
                                     iota_a[:, :].unsqueeze(2).broadcast_to([P, NS, E]), ALU.is_le), l)
                step(V.tensor_reduce(eid[:, :], under[:, :, :], AX_X, ALU.add), l)
                V.tensor_scalar(w_off[:, :], eid[:, :], float(E - 1), float(FF), ALU.min, ALU.mult).then_inc(w_off_ready, 1)
                wide = lambda a: a[:, :].unsqueeze(2).broadcast_to([P, NS, NS])
                step(V.tensor_tensor(on_a[:, :, :], iota_a[:, :].unsqueeze(1).broadcast_to([P, NS, NS]), wide(pos_a),
                                     ALU.is_equal), l)
                step(V.tensor_tensor(place[:, :, 0, :], on_a[:, :, :], wide(source1), ALU.mult), l)
                step(V.tensor_tensor(place[:, :, 1, :], on_a[:, :, :], wide(weight), ALU.mult), l)
                for j in range(NS):
                    V.tensor_scalar(on_b[:, j, :], iota_b[:, :], pos_b[:, j:j + 1], None, ALU.is_equal).then_inc(on_b_ready, 1)
                dve.wait_ge(inv_ready, l + 1)
                V.tensor_scalar(src_i[:, :], ps[6][:, 0:NS], -1.0, 0.0, ALU.add, ALU.max)
                V.tensor_copy(w_found[:, :], ps[6][:, NS:2 * NS])
                V.tensor_scalar(empty[:, :], ps[6][:, 0:NS], 0.0, INVALID, ALU.is_equal, ALU.mult).then_inc(src_ready, 1)
                dve.wait_ge(src_ready, l + 1)
                dve.wait_ge(w_slot_ready, l + 1)
                assert count[0] == ROUTE_STEPS, count[0]

            def experts(l, final=False):
                base = l * NS
                send_rows(l)
                for s in range(NS + 3):
                    t = s - 1
                    if 0 <= t < NS:
                        dve.wait_ge(th_done, base + (t + 1))
                        if t >= 2:
                            dve.wait_ge(hT_in, base + (t - 1))
                        nc.vector.scalar_tensor_tensor(out=act_h[:, t % 2, :], in0=th[:, t % 2, :], scalar=1.0,
                                                       in1=ps[4 + t % 2][:, :], op0=ALU.add, op1=ALU.mult).then_inc(h_done, 1)
                    t = s - 2
                    if 0 <= t < NS:
                        dve.wait_ge(hT_in, base + (t + 1))
                        if t >= 2:
                            dve.wait_ge(y_in, base + (t - 1))
                        nc.vector.tensor_copy(hT[:, t % 2, :, :].rearrange("p c k -> p (c k)"), ps[6 + t % 2][:, :]).then_inc(hT_out, 1)
                    t = s - 3
                    if 0 <= t < NS:
                        dve.wait_ge(y_in, base + (t + 1))
                        if final:
                            nc.vector.scalar_tensor_tensor(out=tok_i[:, t:t + 1], in0=empty[:, t:t + 1], scalar=1000.0,
                                                           in1=xg[:, t, D:D + 1], op0=ALU.mult, op1=ALU.add)
                        elif t % SG == SG - 1:
                            tok = slice(t - SG + 1, t + 1)
                            nc.vector.tensor_copy(y[:, tok, D:ROW], xg[:, tok, D:ROW])
                        nc.vector.tensor_scalar(y[:, t, 0:D], ps[2][:, 0:D], w_slot[:, t:t + 1], None,
                                                ALU.mult).then_inc(y_done, 1)

            experts(0)
            with dve.Fori(1, L - 1) as l:
                experts(l)
            experts(L - 1, final=True)

            for b in range(B):
                k = 2 * B + 1 + b
                tiles = range(TPB * b, TPB * b + TPB)
                dve.wait_ge(got_loaded[b], 16)
                variance(k, lambda t: got[:, t, :], tiles)
                inverse(k, tiles)
                for t in tiles:
                    last = nc.vector.tensor_scalar(got[:, t, :], got[:, t, :], meanvar[:, t, 0:1], rstd[:, t:t + 1],
                                                   ALU.subtract, ALU.mult)
                last.then_inc(ln_out, 1)
                dve.wait_ge(ln_out, 3 * B + b + 1)
                sl = slice(TPB * b, TPB * b + TPB)
                nc.vector.tensor_tensor(got[:, sl, :], got[:, sl, :], x_sb[:, sl, :], ALU.add).then_inc(fin_ready, 1)


_INS = ["L0_attn_x", "L0_attn_q_w", "L0_attn_q_b", "L0_attn_k_w", "L0_attn_k_b", "L0_attn_v_w", "L0_attn_v_b",
        "L0_attn_l_w", "L0_attn_l_b", "L0_ffn_routers", "L0_ffn_W1", "L0_ffn_W2"]


def kernel(**inputs):
    import numpy as np
    import concourse.bacc as bacc
    from concourse.bass_utils import run_bass_kernel_spmd

    nc = bacc.Bacc("TRN2", target_bir_lowering=False, num_devices=1)
    arrays, args = {}, []
    for name in _INS:
        a = np.ascontiguousarray(inputs[name])
        arrays[f"in_{name}"] = a
        args.append(nc.dram_tensor(f"in_{name}", a.shape, mybir.dt.from_np(a.dtype), kind="ExternalInput").ap())
    x = arrays["in_L0_attn_x"]
    args.append(nc.dram_tensor("out", x.shape, F32, kind="ExternalOutput").ap())
    sandwich_kernel(nc, *args)
    r = run_bass_kernel_spmd(nc, [arrays], core_ids=[0])
    return r.results[0]["out"]
```

```python
from contextlib import ExitStack

import concourse.bass as bass
from concourse import mybir

F32 = mybir.dt.float32
F16 = mybir.dt.float16
BF16 = mybir.dt.bfloat16
I32 = mybir.dt.int32
ALU = mybir.AluOpType
ACT = mybir.ActivationFunctionType
AX_X = mybir.AxisListType.X

P = 128
LN_EPS = 1e-5
W_SCALE = 64.0
ROUND = 1.5 * 2.0 ** 23
ROW = P + 2
INVALID = 100.0


def sandwich_kernel(nc, x_in, q_w, q_b, k_w, k_b, v_w, v_b, l_w, l_b, routers, W1, W2, out):
    B, S, D = x_in.shape
    H, DH, _ = q_w.shape
    L, _, E = routers.shape
    FF = W1.shape[2]
    NT = B * S // P
    TPB = S // P
    HD = H * DH
    NPAIR = H // 2
    NP = B * NPAIR
    FC = FF // P
    NS = NT + E - 1
    GROUPS = [range(g, min(g + 8, NS)) for g in range(0, NS, 8)]
    NGR = len(GROUPS)
    HALF = 2048
    assert D == P and DH == 64 and S == 512 and (NS + 1) * E == 512 and FF == 512 and NP // 2 == E and NS * P < 2 * HALF and HALF % P == 0

    x_rows = x_in.rearrange("b (t p) d -> p (b t) d", p=P)
    out_rows = out.rearrange("b (t p) d -> p (b t) d", p=P)
    rows = nc.dram_tensor("rows", [1 + NS * P, ROW], F32, kind="Internal").ap()
    ffn_out = nc.dram_tensor("ffn_out", [NT * P, D], F32, kind="Internal").ap()

    with ExitStack() as ctx:
        def sem(name):
            return ctx.enter_context(nc.semaphore(name))

        def sb(name, shape, dt=F32, of=ctx):
            return of.enter_context(nc.sbuf_tensor(name, shape, dt))

        ident = sb("ident", [P, P])
        eps = sb("eps", [P, 1])
        tok_mem = sb("tok_mem", [P, NT * (D + ROW)])
        x_sb = tok_mem[:, 0:NT * D].rearrange("p (t d) -> p t d", d=D)
        xn = tok_mem[:, NT * D:].rearrange("p (t d) -> p t d", d=ROW)
        stats = sb("stats", [P, NT, 6])
        meanvar = sb("meanvar", [P, NT, 2])
        std = sb("std", [P, NT])
        rstd = sb("rstd", [P, NT])
        w1_sb = sb("w1_sb", [P, E * FF])
        w2_sb = sb("w2_sb", [P, E * FC * D])
        router_sb = sb("router_sb", [P, L * E])
        before = sb("before", [P, P], BF16)
        ones = sb("ones", [P, P], BF16)
        iota_b = sb("iota_b", [P, P], F16)
        iota_a = sb("iota_a", [P, NS])
        label = sb("label", [P, NS])
        one_row = sb("one_row", [P, E])

        att = ctx.enter_context(ExitStack())
        xT_hi = sb("xT_hi", [P, NT * P], F16, att)
        xT_lo = sb("xT_lo", [P, NT * P], F16, att)
        wT_hi = sb("wT_hi", [P, 3, HD], F16, att)
        wT_lo = sb("wT_lo", [P, 3, HD], F16, att)
        lwT = sb("lwT", [P, NPAIR, D], F32, att)
        brow = sb("brow", [2 * NPAIR, P], F32, att)
        bcol = sb("bcol", [P, 2 * NPAIR], F32, att)
        lb_row = sb("lb_row", [1, D], F32, att)
        ones_row = sb("ones_row", [1, P], F32, att)
        vb_all = sb("vb_all", [P, HD], F32, att)
        q_pair = sb("q_pair", [P, 2, 2, S], F16, att)
        k_pair = sb("k_pair", [P, 2, 2, S], F16, att)
        q_stack = sb("q_stack", [P, 2, 2, S], F16, att)
        k_stack = sb("k_stack", [P, 2, 2, 2, S], F16, att)
        v_sb = sb("v_sb", [P, 2, TPB, P], F32, att)
        vp = sb("vp", [P, TPB, P], F32, att)
        e_sb = tok_mem[:, 0:TPB * 2 * S].rearrange("p (t h s) -> p t h s", t=TPB, h=2)
        ctxT = sb("ctxT", [P, NPAIR, B * S], F32, att)
        w_raw = ctxT[:, 0:2, :].rearrange("p a (b j c) -> p (a b) j c", b=2, j=NPAIR)
        mx = sb("mx", [P, TPB, 2], F32, att)
        nmx = sb("nmx", [P, TPB, 2], F32, att)
        minus_sc = sb("minus_sc", [P, 1], F32, att)
        esum = sb("esum", [P, TPB, 2], F32, att)
        rsum = sb("rsum", [P, TPB, 2], F32, att)
        shift = sb("shift", [P, NT], F32, att)
        att_n = xn
        att.close()

        expert_m = sb("expert_m", [P, NS, E])
        xg = sb("xg", [P, NS, ROW])
        on_b = sb("on_b", [P, NS, P], F16)
        on_a = sb("on_a", [P, NS, NS], F16)
        lg = sb("lg", [P, NS, E])
        rel = sb("rel", [P, NS, E])
        cand = sb("cand", [P, NS, E])
        ex = sb("ex", [P, NS, E])
        chosen = sb("chosen", [P, NS, E], BF16)
        part = sb("part", [P, E])
        earlier = sb("earlier", [P, E], BF16)
        ranked = sb("ranked", [P, NS, E])
        first = sb("first", [P, NS, E])
        under = sb("under", [P, NS, E])
        lmax = sb("lmax", [P, NS])
        zsum = sb("zsum", [P, NS])
        weight = sb("weight", [P, NS])
        expert = sb("expert", [P, NS])
        empty = sb("empty", [P, NS])
        rank = sb("rank", [P, NS])
        tile_in = sb("tile_in", [P, NS])
        pos_a = sb("pos_a", [P, NS])
        pos_b = sb("pos_b", [P, NS])
        tiles_e = sb("tiles_e", [P, E])
        cum_e = sb("cum_e", [P, E])
        first_e = sb("first_e", [P, E])
        eid = sb("eid", [P, NS])
        beyond = sb("beyond", [P, NS])
        w_off = sb("w_off", [P, NS], I32)
        src_i = sb("src_i", [P, NS], I32)
        xT = sb("xT", [P, 2, P])
        th = sb("th", [P, 2, FF])
        act_h = sb("act_h", [P, 2, FF])
        hT = sb("hT", [P, 2, FC, P])
        yT = sb("yT", [P, 2, P])
        tok_i = sb("tok_i", [P, NS], I32)
        rowsT = sb("rowsT", [P, 2, S])
        got = sb("got", [P, NT, D])

        ps = [ctx.enter_context(nc.psum_tensor(f"ps{i}", [P, 512], F32)) for i in range(8)]
        ps_ctx, ps_q, ps_k, ps_v = ps[4:8]

        x_loaded = [sem(f"x_loaded{b}") for b in range(B)]
        b_loaded, w_loaded, vb_loaded, ffn_loaded = sem("b_loaded"), sem("w_loaded"), sem("vb_loaded"), sem("ffn_loaded")
        router_loaded = sem("router_loaded")
        consts = sem("consts")
        ln_stat, ln_var, ln_std, ln_rstd, ln_out = sem("ln_stat"), sem("ln_var"), sem("ln_std"), sem("ln_rstd"), sem("ln_out")
        prep_T, prep_hi, prep_done = sem("prep_T"), sem("prep_hi"), sem("prep_done")
        q_ready, k_ready, v_ready = sem("q_ready"), sem("k_ready"), sem("v_ready")
        q_hi, k_hi, q_lo, k_lo = sem("q_hi"), sem("k_hi"), sem("q_lo"), sem("k_lo")
        v_out = sem("v_out")
        q_stacked, k_stacked = [sem("q_stacked0"), sem("q_stacked1")], [sem("k_stacked0"), sem("k_stacked1")]
        scores_ready, max_done, nmax_done, exp_done = sem("scores_ready"), sem("max_done"), sem("nmax_done"), sem("exp_done")
        rsum_done, vp_done, ctx_step, ctx_copied = sem("rsum_done"), sem("vp_done"), sem("ctx_step"), sem("ctx_copied")
        proj_ready, shift_ready, att_done, x1_done = sem("proj_ready"), sem("shift_ready"), sem("att_done"), sem("x1_done")
        xn_T, xn_copied, rows_written = sem("xn_T"), sem("xn_copied"), sem("rows_written")
        numbered, filled = sem("numbered"), sem("filled")
        logits0_ready, lg_copied, rel_ready, exp_ready = sem("logits0_ready"), sem("lg_copied"), sem("rel_ready"), sem("exp_ready")
        chosen_ready, ranks_ready, ranks_read = sem("chosen_ready"), sem("ranks_ready"), sem("ranks_read")
        weight_ready, on_a_ready, on_b_ready, inv_ready = sem("weight_ready"), sem("on_a_ready"), sem("on_b_ready"), sem("inv_ready")
        src_ready, w_off_ready = sem("src_ready"), sem("w_off_ready")
        route = sem("route")
        gathered = [sem(f"gathered{t}") for t in range(NS)]
        xT_in, xT_out, h_in, th_done, h_done = sem("xT_in"), sem("xT_out"), sem("h_in"), sem("th_done"), sem("h_done")
        hT_in, hT_out, y_in, y_done = sem("hT_in"), sem("hT_out"), sem("y_in"), sem("y_done")
        yT_in, yT_out, logit_in = sem("yT_in"), sem("yT_out"), sem("logit_in")
        y_written = sem("y_written")
        tok_ready = sem("tok_ready")
        scattered = sem("scattered")
        got_loaded = [sem(f"got_loaded{b}") for b in range(B)]
        fin_ready, stored = sem("fin_ready"), sem("stored")
        block = ctx.enter_context(nc.Block())

        ps_xT, ps_yT, ps_y, ps_rank = ps[0:4]
        ps_h, ps_hT, ps_inv = ps[4:6], ps[6:8], ps[0]
        ROUTE0_STEPS, ROUTE_STEPS = 21, 65
        ROUTE_AT = [[tiles[-1] + 5 + n for n in range(8)] for tiles in GROUPS[:-1]]
        last_group = GROUPS[-2][-1] + 5
        ROUTE_AT[-1] = [last_group + n for n in (0, 0, 1, 1, 2, 3, 4, 5)]
        RANKS_AT = [at[3] for at in ROUTE_AT]
        EXP_AT = [at[0] for at in ROUTE_AT] + [NS + 99]
        ps_out = [ps_q, ps_k, ps_v, ps_ctx]
        SC = float(DH) ** -0.5 / (W_SCALE * W_SCALE)
        PREP = [("x", b, 0) for b in range(B)] + [("w", m, g) for m in range(4) for g in range(2)]
        NPREP = len(PREP) - 2
        NLN = 3

        @block.sync
        def _(sp):
            for b in range(B):
                sp.dma_start(x_sb[:, b * TPB:(b + 1) * TPB, :], x_rows[:, b * TPB:(b + 1) * TPB, :]).then_inc(x_loaded[b], 16)

            def stack_k(u):
                for hd in range(2):
                    for half in range(2):
                        sp.dma_start(k_stack[64 * half:64 * half + 64, u, hd, :, :],
                                     k_pair[64 * hd:64 * hd + 64, u, :, :]).then_inc(k_stacked[u], 16)

            def stack_q(u):
                for half, hd, hl in ((0, 0, 0), (1, 0, 1), (1, 1, 0), (0, 1, 1)):
                    sp.dma_start(q_stack[64 * half:64 * half + 64, u, hd, :],
                                 q_pair[64 * hd:64 * hd + 64, u, hl, :]).then_inc(q_stacked[u], 16)

            def load_expert(e):
                sp.dma_start(w1_sb[:, bass.ds(e * FF, FF)].unsqueeze(1),
                             W1[bass.ds(e, 1), :, :].rearrange("e d f -> d e f")).then_inc(ffn_loaded, 16)
                sp.dma_start(w2_sb[:, bass.ds(e * FC * D, FC * D)].rearrange("p (c d) -> p c d", c=FC),
                             W2[bass.ds(e, 1), :, :].rearrange("e (c p) d -> p (e c) d", p=P)).then_inc(ffn_loaded, 16)

            for i in range(2):
                sp.wait_ge(k_lo, i + 1)
                stack_k(i)
                sp.wait_ge(q_lo, i + 1)
                stack_q(i)
            load_expert(0)
            with sp.Fori(1, NP // 2) as g:
                scored = [sp.to_reg(16 * g - 8), sp.to_reg(16 * g)]
                written = [sp.to_reg(2 * g + 1), sp.to_reg(2 * g + 2)]
                for u in range(2):
                    sp.wait_ge(scores_ready, scored[u])
                    sp.wait_ge(k_lo, written[u])
                    stack_k(u)
                    sp.wait_ge(q_lo, written[u])
                    stack_q(u)
                load_expert(g)
            sp.wait_ge(ctx_step, 4 * NP)
            for b in range(B):
                sp.dma_start(x_sb[:, b * TPB:(b + 1) * TPB, :], x_rows[:, b * TPB:(b + 1) * TPB, :]).then_inc(x_loaded[b], 16)
            sp.wait_ge(ffn_loaded, 32 * E)
            sp.dma_start(rows[0:1, :], w1_sb[0:1, 0:ROW]).then_inc(rows_written, 16)
            sp.dma_start(rows[1 + NT * P:1 + NS * P, :].rearrange("(t p) d -> p t d", p=P),
                         w1_sb[:, 0:(NS - NT) * ROW].rearrange("p (t d) -> p t d", d=ROW)).then_inc(rows_written, 16)
            sp.wait_ge(numbered, 1)
            sp.wait_ge(weight_ready, 1)
            for b in range(B):
                sp.dma_start(rows[1 + b * S:1 + (b + 1) * S, :].rearrange("(t p) d -> p t d", p=P),
                             xn[:, b * TPB:(b + 1) * TPB, :]).then_inc(rows_written, 16)

            with sp.Fori(0, L - 1) as l:
                weighted = [sp.to_reg(NGR * l + g + 2) for g in range(NGR)]
                sp.wait_ge(xT_in, sp.to_reg(NS * l + NS))
                for g, tiles in enumerate(GROUPS):
                    sp.wait_ge(weight_ready, weighted[g])
                    lo, hi = tiles[0], tiles[-1] + 1
                    sp.dma_start(rows[1 + lo * P:1 + hi * P, :].rearrange("(t p) d -> p t d", p=P),
                                 xg[:, lo:hi, :]).then_inc(y_written, 16)

            sp.wait_ge(scattered, 16 * NS)
            for b in range(B):
                sp.dma_start(got[:, b * TPB:(b + 1) * TPB, :],
                             ffn_out[b * S:(b + 1) * S, :].rearrange("(t p) d -> p t d", p=P)).then_inc(got_loaded[b], 16)
            for b in range(B):
                sp.wait_ge(fin_ready, b + 1)
                sp.dma_start(out_rows[:, b * TPB:(b + 1) * TPB, :], got[:, b * TPB:(b + 1) * TPB, :]).then_inc(stored, 16)
            sp.wait_ge(stored, 16 * B)

        @block.gpsimd
        def _(pool):
            nc.gpsimd.memset(ident[:, :], 0.0).then_inc(consts, 1)
            nc.gpsimd.memset(eps[:, :], LN_EPS).then_inc(consts, 1)
            pool.wait_ge(consts, 2)
            nc.gpsimd.affine_select(out=ident[:, :], in_=ident[:, :], compare_op=ALU.not_equal, fill=1.0,
                                    base=0, pattern=[[-1, P]], channel_multiplier=1).then_inc(consts, 1)
            nc.gpsimd.memset(minus_sc[:, :], -SC).then_inc(consts, 1)
            g = dict(allow_small_or_imprecise_dtypes=True)
            nc.gpsimd.iota(iota_b[:, :], [[1, P]], base=0, channel_multiplier=0, **g).then_inc(consts, 1)
            nc.gpsimd.iota(iota_a[:, :], [[1, NS]], base=0, channel_multiplier=0, **g).then_inc(consts, 1)
            low_tiles = HALF // P
            nc.gpsimd.iota(label[:, 0:low_tiles], [[P, low_tiles]], base=1, channel_multiplier=1, **g).then_inc(consts, 1)
            nc.gpsimd.iota(label[:, low_tiles:NS], [[P, NS - low_tiles]], base=1 - HALF, channel_multiplier=1, **g).then_inc(consts, 1)
            nc.gpsimd.memset(one_row[:, :], 1.0).then_inc(consts, 1)
            nc.gpsimd.memset(ones_row[:, :], 1.0).then_inc(consts, 1)
            nc.gpsimd.memset(ones[:, :], 1.0).then_inc(consts, 1)
            nc.gpsimd.memset(before[:, :], 1.0).then_inc(consts, 1)
            pool.wait_ge(consts, 12)
            nc.gpsimd.affine_select(out=before[:, :], in_=before[:, :], compare_op=ALU.is_ge, fill=0.0,
                                    base=-1, pattern=[[1, P]], channel_multiplier=-1).then_inc(consts, 1)
            pool.dma_start(router_sb[:, :].rearrange("p (l e) -> p l e", l=L),
                           routers.rearrange("l d e -> d l e")).then_inc(router_loaded, 16)
            with pool.Fori(0, NP) as i:
                for n in range(2 * TPB):
                    pool.wait_ge(max_done, 8 * i + (n + 1))
                    nc.gpsimd.tensor_tensor(nmx[:, n // 2, n % 2:n % 2 + 1], mx[:, n // 2, n % 2:n % 2 + 1],
                                            minus_sc[:, :], ALU.mult).then_inc(nmax_done, 1)

            pool.wait_ge(ctx_step, 4 * NP)
            nc.gpsimd.iota(xn[:, :, D:ROW], [[P, NT], [0, ROW - D]], base=0, channel_multiplier=1,
                           allow_small_or_imprecise_dtypes=True).then_inc(numbered, 1)
            pool.wait_ge(proj_ready, B)
            nc.gpsimd.iota(expert_m[:, :, :], [[0, NS], [1, E]], base=-E, channel_multiplier=0,
                           allow_small_or_imprecise_dtypes=True).then_inc(filled, 1)

            def gather(t):
                pool.indirect_dma_start(xg[:, t, :], None, rows, bass.IndirectOffsetOnAxis(ap=src_i[:, t:t + 1], axis=0)
                                        ).then_inc(gathered[t], 16)

            pool.wait_ge(rows_written, 16 * (B + 2))
            pool.wait_ge(src_ready, 1)
            for t in range(NS):
                gather(t)
            with pool.Fori(0, L - 2) as l:
                pool.wait_ge(y_written, 16 * NGR * l + 16 * NGR)
                pool.wait_ge(src_ready, l + 2)
                all_in = pool.to_reg(16 * l + 32)
                for t in range(NS):
                    gather(t)
                pool.wait_ge(gathered[NS - 1], all_in)
            pool.wait_ge(y_written, 16 * NGR * (L - 1))
            pool.wait_ge(src_ready, L)
            for t in range(NS):
                gather(t)
            firsts = [tiles[0] for tiles in GROUPS]
            for t in range(NS):
                if t in firsts:
                    pool.wait_ge(tok_ready, firsts.index(t) + 1)
                pool.wait_ge(y_done, NS * (L - 1) + t + 1)
                pool.indirect_dma_start(ffn_out, bass.IndirectOffsetOnAxis(ap=tok_i[:, t:t + 1], axis=0),
                                        xg[:, t, 0:D], None, bounds_check=NT * P - 1, oob_is_err=False
                                        ).then_inc(scattered, 16)

        @block.tensor
        def _(pe):
            pe.wait_ge(consts, 3)
            pe.wait_ge(b_loaded, 48)
            nb = 2 * NPAIR
            nc.tensor.transpose(ps_v[:, 0:nb], brow[:, :], ident[0:nb, 0:nb]).then_inc(prep_T, 1)
            def prepare(n):
                kind, m, g = PREP[n]
                if n >= 4:
                    pe.wait_ge(prep_done, n - 3 + 1)
                if n == B:
                    pe.wait_ge(w_loaded, 16 * 4)
                if kind == "x":
                    pe.wait_ge(ln_out, m + 1)
                for c in range(4):
                    src_ = w_raw[:, m, 4 * g + c, :] if kind == "w" else xn[:, TPB * m + c, 0:D]
                    last = nc.tensor.transpose(ps[n % 4][:, c * P:(c + 1) * P], src_, ident[:, :])
                last.then_inc(prep_T, 1)

            for n in range(NPREP):
                prepare(n)

            PASSES = [(wT_hi, xT_hi), (wT_lo, xT_hi), (wT_hi, xT_lo)]

            def project_qk(dst, m, tok, pair):
                for n, (w, x) in enumerate(PASSES):
                    last = nc.tensor.matmul(dst[:, :], w[:, m, bass.ds(pair * P, P)], x[:, bass.ds(tok, S)],
                                            start=(n == 0), stop=(n == 2))
                return last

            def project_v(tok, pair):
                for t in range(TPB):
                    for n, (w, x) in enumerate(PASSES):
                        last = nc.tensor.matmul(ps_v[:, t * P:(t + 1) * P], x[:, bass.ds(tok + t * P, P)],
                                                w[:, 2, bass.ds(pair * P, P)], start=(n == 0), stop=(n == 2))
                return last

            def scores(i, u, kt, first):
                if kt == 0:
                    pe.wait_ge(q_stacked[u], 32 * i + (64 - 32 * u))
                    pe.wait_ge(k_stacked[u], 32 * i + (64 - 32 * u))
                for hd in range(2):
                    n = 2 * kt + hd
                    if not (first and n < 4):
                        pe.wait_ge(exp_done, 8 * i + (n - 3))
                    for hl in range(2):
                        last = nc.tensor.matmul(ps[n % 4][:, :], k_stack[:, u, hd, hl, kt * P:(kt + 1) * P],
                                                q_stack[:, u, hd, :], start=(hl == 0), stop=(hl == 1))
                    last.then_inc(scores_ready, 1)

            def context(i, kt, first=False):
                if kt == 0 and not first:
                    pe.wait_ge(ctx_copied, i)
                pe.wait_ge(vp_done, 4 * i + (kt + 1))
                for hd in range(2):
                    last = nc.tensor.matmul(ps_ctx[64 * hd:64 * hd + 64, :], vp[:, kt, 64 * hd:64 * hd + 64],
                                            e_sb[:, kt, hd, :], start=(kt == 0), stop=(kt == TPB - 1))
                last.then_inc(ctx_step, 1)

            def pair_step(i, u, first=False, second=False, ahead=2):
                for kt in range(TPB):
                    scores(i, u, kt, first)
                    if ahead >= 1 and kt == 2:
                        pe.wait_ge(v_out, i + 1)
                        project_v(((i + 1) // NPAIR) * S, (i + 1) % NPAIR).then_inc(v_ready, 1)
                    if ahead >= 2 and kt == 0:
                        pe.wait_ge(k_lo, i + 2)
                        project_qk(ps_k, 1, ((i + 2) // NPAIR) * S, (i + 2) % NPAIR).then_inc(k_ready, 1)
                    if ahead >= 2 and kt == 1:
                        pe.wait_ge(q_lo, i + 2)
                        project_qk(ps_q, 0, ((i + 2) // NPAIR) * S, (i + 2) % NPAIR).then_inc(q_ready, 1)
                    if not first:
                        context(i - 1, kt, first=second)

            pe.wait_ge(prep_done, NPREP + 1)
            project_qk(ps_k, 1, 0, 0).then_inc(k_ready, 1)
            project_qk(ps_q, 0, 0, 0).then_inc(q_ready, 1)
            project_v(0, 0).then_inc(v_ready, 1)
            pe.wait_ge(k_lo, 1)
            project_qk(ps_k, 1, 0, 1).then_inc(k_ready, 1)
            pe.wait_ge(q_lo, 1)
            project_qk(ps_q, 0, 0, 1).then_inc(q_ready, 1)
            for n in range(NPREP, len(PREP)):
                prepare(n)
            pe.wait_ge(prep_done, len(PREP) + 1)
            pair_step(0, 0, first=True)
            pair_step(1, 1, second=True)
            with pe.Fori(1, NP // 2 - 1) as g:
                for u in range(2):
                    pair_step(2 * g + u, u)
            pair_step(NP - 2, 0, ahead=1)
            pair_step(NP - 1, 1, ahead=0)

            def project_out(b):
                pe.wait_ge(ctx_copied, NPAIR * (b + 1))
                for c in range(TPB):
                    for j in range(NPAIR):
                        nc.tensor.matmul(ps_out[b][:, c * D:(c + 1) * D], ctxT[:, j, b * S + c * P:b * S + (c + 1) * P],
                                         lwT[:, j, :], start=(j == 0), stop=False)
                    last = nc.tensor.matmul(ps_out[b][:, c * D:(c + 1) * D], ones_row[:, :], lb_row[:, :], start=False, stop=True)
                last.then_inc(proj_ready, 1)

            def logits(b):
                pe.wait_ge(ln_out, B + b + 1)
                for c in range(TPB):
                    last = nc.tensor.transpose(ps[2][:, c * P:(c + 1) * P], xn[:, b * TPB + c, 0:D], ident[:, :])
                last.then_inc(xn_T, 1)
                pe.wait_ge(xn_copied, b + 1)
                for c in range(TPB):
                    j = b * TPB + c
                    last = nc.tensor.matmul(ps[1][:, j * E:(j + 1) * E], rowsT[:, b % 2, c * P:(c + 1) * P],
                                            router_sb[:, 0:E], start=True, stop=True)
                return last

            project_out(0)
            for kt in range(TPB):
                context(NP - 1, kt)
            pe.wait_ge(ffn_loaded, 32 * E)
            pe.wait_ge(router_loaded, 16)
            for b in range(1, B):
                project_out(b)
                if b >= 2:
                    logits(b - 2)
            logits(B - 2)
            logits(B - 1).then_inc(logits0_ready, 1)

            def count_ranks(tiles, carry, total):
                end = NS * E + E if total else (tiles[-1] + 1) * E
                by_tile = lambda j: ps_rank[:, j * E:end].rearrange("p (j e) -> p j e", e=E)
                bcast = lambda a, j: a.unsqueeze(1).broadcast_to([P, end // E - j, E])
                if carry:
                    nc.tensor.matmul(by_tile(tiles[0]), ones[:, :], bcast(earlier[:, :], tiles[0]), start=True, stop=False)
                for j in tiles:
                    last = nc.tensor.matmul(ps_rank[:, j * E:(j + 1) * E], before[:, :], chosen[:, j, :],
                                            start=(j == tiles[0] and not carry), stop=(j == tiles[-1] and not total))
                    if (j + 1) * E < end:
                        last = nc.tensor.matmul(by_tile(j + 1), ones[:, :], bcast(chosen[:, j, :], j + 1),
                                                start=False, stop=(j == tiles[-1]))
                return last

            def invert(tiles, count, last_group):
                half = len(tiles) // 2
                for j in tiles:
                    if j in (0, half):
                        pe.wait_ge(on_a_ready, 2 * count - (j == 0))
                    if j == last_group:
                        pe.wait_ge(on_b_ready, count)
                    last = nc.tensor.matmul(ps_inv[:, 0:NS], on_b[:, j, :], on_a[:, j, :], start=(j == 0), stop=(j == tiles[-1]))
                last.then_inc(inv_ready, 1)

            pe.wait_ge(chosen_ready, 1)
            count_ranks(range(NT), False, True).then_inc(ranks_ready, 1)
            invert(range(NT), 1, 0)

            OG = 8
            offs = [pe.alloc_register(f"w_off{t}") for t in range(2 * OG)]

            def experts(l, final=False):
                base = l * NS
                pe.wait_ge(w_off_ready, l + 1)
                first_in = pe.to_reg(16 * l + 16)
                off = {}
                for s in range(-1, NS + (2 if final else 4)):
                    if (s + 1) % OG == 0 and s + 1 < NS:
                        lo, hi = s + 1, min(s + 1 + OG, NS)
                        half = (lo // OG) % 2 * OG
                        pe.load(offs[half:half + hi - lo], w_off[0:1, lo:hi])
                        for t in range(lo, hi):
                            off[t] = pe.snap(offs[half + t - lo], min_val=0, max_val=(E - 1) * FF)
                    t = s
                    if 0 <= t < NS:
                        pe.wait_ge(xT_out, base + (t + 1))
                        if t >= 2:
                            pe.wait_ge(h_done, base + (t - 1))
                        nc.tensor.matmul(ps_h[t % 2][:, :], xT[:, t % 2, :], w1_sb[:, bass.ds(off[t], FF)],
                                         start=True, stop=True).then_inc(h_in, 1)
                    t = s + 1
                    if t < NS:
                        pe.wait_ge(gathered[t], first_in if t == 0 else 16 * l + 16)
                        if t > 0:
                            pe.wait_ge(xT_out, base + t)
                        nc.tensor.transpose(ps_xT[:, 0:P], xg[:, t, 0:D], ident[:, :]).then_inc(xT_in, 1)
                    t = s - 1
                    if 0 <= t < NS:
                        pe.wait_ge(h_done, base + (t + 1))
                        if t >= 2:
                            pe.wait_ge(hT_out, base + (t - 1))
                        for c in range(FC):
                            last = nc.tensor.transpose(ps_hT[t % 2][:, c * P:(c + 1) * P],
                                                       act_h[:, t % 2, c * P:(c + 1) * P], ident[:, :])
                        last.then_inc(hT_in, 1)
                    t = s - 2
                    if 0 <= t < NS:
                        pe.wait_ge(hT_out, base + (t + 1))
                        if t > 0:
                            pe.wait_ge(y_done, base + t)
                        for c in range(FC):
                            last = nc.tensor.matmul(ps_y[:, 0:D], hT[:, t % 2, c, :],
                                                    w2_sb[:, bass.ds(off[t] + c * D, D)], start=(c == 0), stop=(c == FC - 1))
                        last.then_inc(y_in, 1)
                    if final:
                        continue
                    t = s - 4
                    if 0 <= t < NS:
                        pe.wait_ge(yT_out, base + (t + 1))
                        if t > 0:
                            pe.wait_ge(lg_copied, base + t + 1)
                        nc.tensor.matmul(ps_yT[:, P:P + E], yT[:, t % 2, :], router_sb[:, bass.ds((l + 1) * E, E)],
                                         start=True, stop=True).then_inc(logit_in, 1)
                    t = s - 3
                    if 0 <= t < NS:
                        pe.wait_ge(y_done, base + (t + 1))
                        nc.tensor.transpose(ps_yT[:, 0:P], xg[:, t, 0:D], ident[:, :]).then_inc(yT_in, 1)
                    for g in range(NGR - 1):
                        if s == RANKS_AT[g] + 1:
                            ranks(l, g)

            def ranks(l, g):
                pe.wait_ge(chosen_ready, NGR * l + g + 2)
                if g > 0:
                    pe.wait_ge(ranks_read, (NGR - 1) * l + g)
                count_ranks(GROUPS[g], g > 0, g == NGR - 1).then_inc(ranks_ready, 1)

            with pe.Fori(0, L - 1) as l:
                experts(l)
                ranks(l, NGR - 1)
                invert(range(NS), l + 2, GROUPS[-1][0])
            experts(L - 1, final=True)

        @block.scalar
        def _(act):
            for m, (dst, bias) in enumerate(((0, q_b), (NPAIR, k_b))):
                act.dma_start(brow[dst:dst + NPAIR, :], bias.rearrange("(j r) o p -> j (r o p)", r=2)).then_inc(b_loaded, 16)
            act.dma_start(lb_row[:, :], l_b).then_inc(b_loaded, 16)
            for m, w in enumerate((q_w, k_w, v_w)):
                act.dma_start(w_raw[:, m], w.rearrange("(j r) p d -> (r p) j d", r=2)).then_inc(w_loaded, 16)
            act.dma_start(w_raw[:, 3], l_w.rearrange("o (j p) -> o j p", p=P)).then_inc(w_loaded, 16)
            act.dma_start(vb_all[:, :], v_b.rearrange("h o p -> o (h p)").broadcast_to([P, HD])).then_inc(vb_loaded, 16)

            act.wait_ge(consts, 2)

            def sqrt(k):
                act.wait_ge(ln_var, k + 1)
                if k == 0:
                    sl = slice(0, NT)
                else:
                    b_ = (k - 1) // 2 if k <= 2 * B else k - 2 * B - 1
                    sl = slice(TPB * b_, TPB * b_ + TPB)
                nc.scalar.activation(std[:, sl], meanvar[:, sl, 1], ACT.Sqrt, bias=eps[:, 0:1]).then_inc(ln_std, 1)

            sqrt(0)
            for n, (kind, m, g) in enumerate(PREP[:NPREP]):
                act.wait_ge(prep_T, n + 2)
                if kind == "w":
                    nc.scalar.activation(wT_hi[:, m, 512 * g:512 * g + 512], ps[n % 4][:, :], ACT.Copy,
                                         scale=W_SCALE).then_inc(prep_hi, 1)
                else:
                    nc.scalar.activation(xT_hi[:, S * m:S * m + S], ps[n % 4][:, :], ACT.Copy).then_inc(prep_hi, 1)

            def high(dst, u, src_, ready, done, stacked, i, col):
                act.wait_ge(ready, i + 1)
                if stacked is not None:
                    act.wait_ge(stacked[u], 32 * i - 32 * u)
                nc.scalar.activation(dst[:, u, 0, :], src_[:, :], ACT.Identity, bias=bcol[:, bass.ds(col, 1)]).then_inc(done, 1)

            def k_high(i, u, pair, first=False):
                high(k_pair, u, ps_k, k_ready, k_hi, None if first else k_stacked, i, pair + NPAIR)

            def q_high(i, u, pair, first=False):
                high(q_pair, u, ps_q, q_ready, q_hi, None if first else q_stacked, i, pair)

            def copy_context(i):
                act.wait_ge(ctx_step, 4 * i + 4)
                flat = ctxT[:, :, :].rearrange("p j t -> p (j t)")
                nc.scalar.activation(flat[:, bass.ds((i % NPAIR) * (B * S) + (i // NPAIR) * S, S)], ps_ctx[:, :],
                                     ACT.Copy).then_inc(ctx_copied, 1)

            def pair_step(i, u, first=False, project=True):
                for kt in range(TPB):
                    if not first:
                        act.wait_ge(ctx_step, 4 * i + (kt - 3))
                    for hd in range(2):
                        act.wait_ge(nmax_done, 8 * i + (2 * kt + hd + 1))
                        nc.scalar.activation(e_sb[:, kt, hd, :], ps[(2 * kt + hd) % 4][:, :], ACT.Exp,
                                             bias=nmx[:, kt, hd:hd + 1], scale=SC,
                                             accum_out=esum[:, kt, hd:hd + 1]).then_inc(exp_done, 1)
                        if not first and kt == TPB - 1 and hd == 0:
                            copy_context(i - 1)
                    if project and kt == 1:
                        k_high(i + 2, u, (i + 2) % NPAIR)
                    if project and kt == 2:
                        q_high(i + 2, u, (i + 2) % NPAIR)
            act.wait_ge(prep_done, 1)
            for i in range(2):
                k_high(i, i, i, first=True)
                q_high(i, i, i, first=True)
            pair_step(0, 0, first=True)
            pair_step(1, 1)
            with act.Fori(1, NP // 2 - 1) as g:
                for u in range(2):
                    pair_step(2 * g + u, u)
            pair_step(NP - 2, 0, project=False)
            pair_step(NP - 1, 1, project=False)
            copy_context(NP - 1)

            def copy_rows(b):
                act.wait_ge(xn_T, b + 1)
                nc.scalar.activation(rowsT[:, b % 2, :], ps[2][:, :], ACT.Copy).then_inc(xn_copied, 1)

            def normalise(b):
                sqrt(2 * b + 1)
                act.wait_ge(shift_ready, b + 1)
                for t in range(TPB * b, TPB * b + TPB):
                    last = nc.scalar.activation(att_n[:, t, 0:D], ps_out[b][:, (t % TPB) * D:(t % TPB + 1) * D], ACT.Identity,
                                                bias=shift[:, t:t + 1], scale=rstd[:, t:t + 1])
                last.then_inc(att_done, 1)
                sqrt(2 * b + 2)

            normalise(0)
            for b in range(1, B):
                normalise(b)
                copy_rows(b - 1)
            copy_rows(B - 1)
            act.wait_ge(logits0_ready, 1)
            nc.scalar.activation(lg[:, 0:NT, :].rearrange("p j e -> p (j e)"), ps[1][:, 0:NT * E], ACT.Copy).then_inc(lg_copied, 1)

            def exponentials(tiles, count):
                act.wait_ge(rel_ready, count)
                sl = slice(tiles[0], tiles[-1] + 1)
                nc.scalar.activation(ex[:, sl, :], rel[:, sl, :], ACT.Exp).then_inc(exp_ready, 1)

            exponentials(range(NT), 1)

            def experts(l, final=False):
                base = l * NS
                for s in range(-1, NS + (2 if final else 4)):
                    t = s
                    if 0 <= t < NS:
                        act.wait_ge(h_in, base + (t + 1))
                        if t >= 2:
                            act.wait_ge(h_done, base + (t - 1))
                        nc.scalar.activation(th[:, t % 2, :], ps_h[t % 2][:, :], ACT.Tanh, scale=0.5).then_inc(th_done, 1)
                    t = s + 1
                    if t < NS:
                        act.wait_ge(xT_in, base + (t + 1))
                        if t >= 2:
                            act.wait_ge(h_in, base + (t - 1))
                        nc.scalar.activation(xT[:, t % 2, :], ps_xT[:, 0:P], ACT.Copy).then_inc(xT_out, 1)
                    t = s - 2
                    if 0 <= t < NS:
                        act.wait_ge(y_in, base + (t + 1))
                        nc.scalar.activation(xg[:, t, 0:D], ps_y[:, 0:D], ACT.Copy,
                                             scale=xg[:, t, D + 1:D + 2]).then_inc(y_done, 1)
                    if final:
                        continue
                    t = s - 3
                    if 0 <= t < NS:
                        act.wait_ge(yT_in, base + (t + 1))
                        if t >= 2:
                            act.wait_ge(logit_in, base + (t - 1))
                        nc.scalar.activation(yT[:, t % 2, :], ps_yT[:, 0:P], ACT.Copy).then_inc(yT_out, 1)
                    t = s - 4
                    if 0 <= t < NS:
                        act.wait_ge(logit_in, base + (t + 1))
                        nc.scalar.activation(lg[:, t, :], ps_yT[:, P:P + E], ACT.Copy).then_inc(lg_copied, 1)
                    for g in range(NGR):
                        if s == EXP_AT[g] + 1:
                            exponentials(GROUPS[g], NGR * l + g + 2)

            with act.Fori(0, L - 1) as l:
                experts(l)
                exponentials(GROUPS[NGR - 1], NGR * l + NGR + 1)
            experts(L - 1, final=True)
            for b in range(B):
                sqrt(2 * B + 1 + b)

        @block.vector
        def _(dve):
            def variance(k, rows_of, tiles):
                for t in tiles:
                    last = nc.vector.bn_stats(stats[:, t, :], rows_of(t))
                last.then_inc(ln_stat, 1)
                dve.wait_ge(ln_stat, k + 1)
                for t in tiles:
                    last = nc.vector.bn_aggr(meanvar[:, t, :], stats[:, t, :])
                last.then_inc(ln_var, 1)

            def inverse(k, tiles):
                dve.wait_ge(ln_std, k + 1)
                sl = slice(tiles[0], tiles[-1] + 1)
                nc.vector.reciprocal(rstd[:, sl], std[:, sl]).then_inc(ln_rstd, 1)
                dve.wait_ge(ln_rstd, k + 1)

            for b in range(B):
                dve.wait_ge(x_loaded[b], 16)
                for t in range(TPB * b, TPB * b + TPB):
                    last = nc.vector.bn_stats(stats[:, t, :], x_sb[:, t, :])
            last.then_inc(ln_stat, 1)
            dve.wait_ge(ln_stat, 1)
            for t in range(NT):
                last = nc.vector.bn_aggr(meanvar[:, t, :], stats[:, t, :])
            last.then_inc(ln_var, 1)
            dve.wait_ge(prep_T, 1)
            nc.vector.tensor_scalar(bcol[:, :], ps_v[:, 0:2 * NPAIR], W_SCALE, None, ALU.mult).then_inc(prep_done, 1)
            inverse(0, range(NT))
            for b in range(B):
                for t in range(TPB * b, TPB * b + TPB):
                    last = nc.vector.tensor_scalar(xn[:, t, 0:D], x_sb[:, t, :], meanvar[:, t, 0:1],
                                                   rstd[:, t:t + 1], ALU.subtract, ALU.mult)
                last.then_inc(ln_out, 1)
            for n, (kind, m, g) in enumerate(PREP[:NPREP]):
                dve.wait_ge(prep_hi, n + 1)
                if kind == "w":
                    nc.vector.scalar_tensor_tensor(out=wT_lo[:, m, 512 * g:512 * g + 512], in0=ps[n % 4][:, :],
                                                   scalar=W_SCALE, in1=wT_hi[:, m, 512 * g:512 * g + 512],
                                                   op0=ALU.mult, op1=ALU.subtract).then_inc(prep_done, 1)
                else:
                    nc.vector.tensor_tensor(xT_lo[:, S * m:S * m + S], ps[n % 4][:, :], xT_hi[:, S * m:S * m + S],
                                            ALU.subtract).then_inc(prep_done, 1)

            def low(dst, u, src_, hi, done, col, i):
                dve.wait_ge(hi, i + 1)
                nc.vector.scalar_tensor_tensor(out=dst[:, u, 1, :], in0=src_[:, :], scalar=bcol[:, bass.ds(col, 1)],
                                               in1=dst[:, u, 0, :], op0=ALU.add, op1=ALU.subtract).then_inc(done, 1)

            def values(i, u, pair):
                dve.wait_ge(v_ready, i + 1)
                nc.vector.scalar_tensor_tensor(
                    out=v_sb[:, u, :, :], in0=ps_v[:, :].rearrange("p (t c) -> p t c", t=TPB), scalar=1.0 / W_SCALE,
                    in1=vb_all[:, bass.ds(pair * P, P)].unsqueeze(1).broadcast_to([P, TPB, P]),
                    op0=ALU.mult, op1=ALU.add).then_inc(v_out, 1)

            def scale_values(i, u, kt):
                dve.wait_ge(exp_done, 8 * i + (2 * kt + 2))
                nc.vector.reciprocal(rsum[:, kt, :], esum[:, kt, :]).then_inc(rsum_done, 1)
                dve.wait_ge(rsum_done, 4 * i + (kt + 1))
                nc.vector.tensor_tensor(vp[:, kt, :].rearrange("p (h c) -> p h c", h=2),
                                        v_sb[:, u, kt, :].rearrange("p (h c) -> p h c", h=2),
                                        rsum[:, kt, :].unsqueeze(2).broadcast_to([P, 2, DH]),
                                        ALU.mult).then_inc(vp_done, 1)

            def pair_step(i, u, ahead=2, first=False):
                for kt in range(TPB):
                    for hd in range(2):
                        dve.wait_ge(scores_ready, 8 * i + (2 * kt + hd + 1))
                        nc.vector.tensor_reduce(mx[:, kt, hd:hd + 1], ps[(2 * kt + hd) % 4][:, :], AX_X,
                                                ALU.max).then_inc(max_done, 1)
                    if kt >= 1:
                        scale_values(i, u, kt - 1)
                    elif not first:
                        scale_values(i - 1, 1 - u, TPB - 1)
                    if kt == 0 and not first:
                        values(i, u, i % NPAIR)
                    if ahead >= 2 and kt == 2:
                        low(k_pair, u, ps_k, k_hi, k_lo, (i + 2) % NPAIR + NPAIR, i + 2)
                    if ahead >= 2 and kt == 3:
                        low(q_pair, u, ps_q, q_hi, q_lo, (i + 2) % NPAIR, i + 2)

            low(k_pair, 0, ps_k, k_hi, k_lo, NPAIR, 0)
            low(q_pair, 0, ps_q, q_hi, q_lo, 0, 0)
            dve.wait_ge(vb_loaded, 16)
            values(0, 0, 0)
            low(k_pair, 1, ps_k, k_hi, k_lo, NPAIR + 1, 1)
            low(q_pair, 1, ps_q, q_hi, q_lo, 1, 1)
            for n in range(NPREP, len(PREP)):
                _, m, g = PREP[n]
                dve.wait_ge(prep_T, n + 2)
                nc.vector.tensor_copy(lwT[:, 4 * g:4 * g + 4, :].rearrange("p a b -> p (a b)"),
                                      ps[n % 4][:, :]).then_inc(prep_done, 1)
            pair_step(0, 0, first=True)
            pair_step(1, 1)
            with dve.Fori(1, NP // 2 - 1) as g:
                for u in range(2):
                    pair_step(2 * g + u, u)
            pair_step(NP - 2, 0, ahead=1)
            pair_step(NP - 1, 1, ahead=0)
            scale_values(NP - 1, 1, TPB - 1)

            for b in range(B):
                tiles = range(TPB * b, TPB * b + TPB)
                k = 1 + 2 * b
                dve.wait_ge(proj_ready, b + 1)
                variance(k, lambda t: ps_out[b][:, (t % TPB) * P:(t % TPB + 1) * P], tiles)
                inverse(k, tiles)
                sl = slice(TPB * b, TPB * b + TPB)
                nc.vector.scalar_tensor_tensor(out=shift[:, sl], in0=meanvar[:, sl, 0], scalar=-1.0, in1=rstd[:, sl],
                                               op0=ALU.mult, op1=ALU.mult).then_inc(shift_ready, 1)
                dve.wait_ge(att_done, b + 1)
                dve.wait_ge(x_loaded[b], 32)
                nc.vector.tensor_tensor(x_sb[:, sl, :], x_sb[:, sl, :], att_n[:, sl, 0:D], ALU.add).then_inc(x1_done, 1)
                dve.wait_ge(x1_done, b + 1)
                variance(k + 1, lambda t: x_sb[:, t, :], tiles)
                inverse(k + 1, tiles)
                for t in tiles:
                    last = nc.vector.tensor_scalar(xn[:, t, 0:D], x_sb[:, t, :], meanvar[:, t, 0:1],
                                                   rstd[:, t:t + 1], ALU.subtract, ALU.mult)
                last.then_inc(ln_out, 1)

            count = [0]

            def step(ins, base):
                count[0] += 1
                ins.then_inc(route, 1)
                dve.wait_ge(route, base + count[0])

            def pair(one, other, base):
                one.then_inc(route, 1)
                count[0] += 1
                step(other, base)

            V = nc.vector

            def best(n, sl, base, lgs, rels, experts_=None):
                w = sl.stop - sl.start
                if n == 0:
                    dve.wait_ge(lg_copied, lgs)
                    step(V.tensor_reduce(lmax[:, sl], lg[:, sl, :], AX_X, ALU.max), base)
                    V.tensor_tensor(rel[:, sl, :], lg[:, sl, :], lmax[:, sl].unsqueeze(2).broadcast_to([P, w, E]),
                                    ALU.subtract).then_inc(rel_ready, 1)
                    dve.wait_ge(rel_ready, rels)
                elif n == 1:
                    step(V.scalar_tensor_tensor(out=cand[:, sl, :], in0=rel[:, sl, :], scalar=0.0, in1=expert_m[:, sl, :],
                                                op0=ALU.is_equal, op1=ALU.mult), base)
                elif n == 2:
                    step(V.tensor_reduce(expert[:, sl], cand[:, sl, :], AX_X, ALU.min), base)
                    if experts_ is None:
                        step(V.tensor_tensor(expert[:, sl], expert[:, sl], empty[:, sl], ALU.add), base)
                elif n == 3:
                    V.tensor_tensor(chosen[:, sl, :], expert_m[:, sl, :], expert[:, sl].unsqueeze(2).broadcast_to([P, w, E]),
                                    ALU.is_equal).then_inc(chosen_ready, 1)

            def weights(sl, base, rels, rows_):
                dve.wait_ge(exp_ready, rels)
                step(V.tensor_reduce(zsum[:, sl], ex[:, sl, :], AX_X, ALU.add), base)
                step(V.reciprocal(weight[:, sl], zsum[:, sl]), base)
                V.tensor_scalar(rows_[:, sl, D + 1], weight[:, sl], 0.5, None, ALU.mult).then_inc(weight_ready, 1)

            def places(n, sl, base, reads, counts):
                if n == 0:
                    dve.wait_ge(ranks_ready, counts)
                    V.tensor_tensor(ranked[:, sl, :], ps_rank[:, sl.start * E:sl.stop * E].rearrange("p (j e) -> p j e", e=E),
                                    chosen[:, sl, :], ALU.mult).then_inc(ranks_read, 1)
                    dve.wait_ge(ranks_read, reads)
                    step(V.tensor_reduce(rank[:, sl], ranked[:, sl, :], AX_X, ALU.add), base)
                elif n == 1:
                    step(V.tensor_scalar(tile_in[:, sl], rank[:, sl], -(P - 1) / 2.0, 1.0 / P, ALU.add, ALU.mult), base)
                    step(V.tensor_scalar(tile_in[:, sl], tile_in[:, sl], ROUND, ROUND, ALU.add, ALU.subtract), base)
                    step(V.scalar_tensor_tensor(out=pos_b[:, sl], in0=tile_in[:, sl], scalar=-float(P), in1=rank[:, sl],
                                                op0=ALU.mult, op1=ALU.add), base)
                    step(V.tensor_tensor(tile_in[:, sl], tile_in[:, sl], empty[:, sl], ALU.add), base)
                elif n == 2:
                    step(one_hots(sl), base)

            def one_hots(sl):
                for j in range(sl.start, sl.stop):
                    last = V.tensor_scalar(on_b[:, j, :], iota_b[:, :], pos_b[:, j:j + 1], label[:, j:j + 1],
                                           ALU.is_equal, ALU.mult)
                return last

            def finish(sl, base, counts, l, all_real=False):
                n = sl.stop
                dve.wait_ge(ranks_ready, counts)
                pair(V.tensor_tensor(ranked[:, sl, :], ps_rank[:, sl.start * E:sl.stop * E].rearrange("p (j e) -> p j e", e=E),
                                     chosen[:, sl, :], ALU.mult),
                     V.tensor_scalar(tiles_e[:, :], ps_rank[:, NS * E:], (P - 1) / 2.0, 1.0 / P, ALU.add, ALU.mult), base)
                pair(V.tensor_reduce(rank[:, sl], ranked[:, sl, :], AX_X, ALU.add),
                     V.tensor_scalar(tiles_e[:, :], tiles_e[:, :], ROUND, ROUND, ALU.add, ALU.subtract), base)
                pair(V.tensor_scalar(tile_in[:, sl], rank[:, sl], -(P - 1) / 2.0, 1.0 / P, ALU.add, ALU.mult),
                     V.tensor_tensor_scan(cum_e[:, :], one_row[:, :], tiles_e[:, :], 0.0, ALU.mult, ALU.add), base)
                pair(V.tensor_scalar(tile_in[:, sl], tile_in[:, sl], ROUND, ROUND, ALU.add, ALU.subtract),
                     V.tensor_tensor(first_e[:, :], cum_e[:, :], tiles_e[:, :], ALU.subtract), base)
                pair(V.scalar_tensor_tensor(out=pos_b[:, sl], in0=tile_in[:, sl], scalar=-float(P), in1=rank[:, sl],
                                            op0=ALU.mult, op1=ALU.add),
                     V.tensor_tensor(first[:, 0:n, :], chosen[:, 0:n, :], first_e[:, :].unsqueeze(1).broadcast_to([P, n, E]),
                                     ALU.mult), base)
                if all_real:
                    step(V.tensor_reduce(pos_a[:, 0:n], first[:, 0:n, :], AX_X, ALU.add), base)
                else:
                    pair(V.tensor_tensor(tile_in[:, sl], tile_in[:, sl], empty[:, sl], ALU.add),
                         V.tensor_reduce(pos_a[:, 0:n], first[:, 0:n, :], AX_X, ALU.add), base)
                step(V.tensor_tensor(pos_a[:, 0:n], pos_a[:, 0:n], tile_in[:, 0:n], ALU.add), base)
                for lo, hi in ((0, n // 2), (n // 2, n)):
                    V.tensor_tensor(on_a[:, lo:hi, :], iota_a[:, :].unsqueeze(1).broadcast_to([P, hi - lo, NS]),
                                    pos_a[:, lo:hi].unsqueeze(2).broadcast_to([P, hi - lo, NS]),
                                    ALU.is_equal).then_inc(on_a_ready, 1)
                one_hots(sl).then_inc(on_b_ready, 1)
                step(V.tensor_tensor(under[:, :, :], cum_e[:, :].unsqueeze(1).broadcast_to([P, NS, E]),
                                     iota_a[:, :].unsqueeze(2).broadcast_to([P, NS, E]), ALU.is_le), base)
                step(V.tensor_reduce(eid[:, :], under[:, :, :], AX_X, ALU.add), base)
                dve.wait_ge(inv_ready, l + 1)
                step(V.tensor_scalar(beyond[:, :], ps_inv[:, 0:NS], 0.0, 2.0 * HALF, ALU.is_lt, ALU.mult), base)
                V.tensor_tensor(src_i[:, :], ps_inv[:, 0:NS], beyond[:, :], ALU.add).then_inc(src_ready, 1)
                step(V.tensor_scalar(empty[:, :], ps_inv[:, 0:NS], 0.0, INVALID, ALU.is_equal, ALU.mult), base)
                V.tensor_scalar(w_off[:, :], eid[:, :], float(E - 1), float(FF), ALU.min, ALU.mult).then_inc(w_off_ready, 1)

            def experts(l, final=False):
                base = l * NS
                for s in range(NS + (2 if final else 4)):
                    t = s - 1
                    if 0 <= t < NS:
                        dve.wait_ge(hT_in, base + (t + 1))
                        if t >= 2:
                            dve.wait_ge(y_in, base + (t - 1))
                        V.tensor_copy(hT[:, t % 2, :, :].rearrange("p c k -> p (c k)"), ps_hT[t % 2][:, :]).then_inc(hT_out, 1)
                    t = s
                    if t < NS:
                        dve.wait_ge(th_done, base + (t + 1))
                        if t >= 2:
                            dve.wait_ge(hT_in, base + (t - 1))
                        V.scalar_tensor_tensor(out=act_h[:, t % 2, :], in0=th[:, t % 2, :], scalar=1.0,
                                               in1=ps_h[t % 2][:, :], op0=ALU.add, op1=ALU.mult).then_inc(h_done, 1)
                    if final:
                        for g in [tiles for tiles in GROUPS if s == tiles[-1] - 1]:
                            dve.wait_ge(xT_in, base + (s + 2))
                            V.scalar_tensor_tensor(out=tok_i[:, g[0]:g[-1] + 1], in0=empty[:, g[0]:g[-1] + 1], scalar=1000.0,
                                                   in1=xg[:, g[0]:g[-1] + 1, D], op0=ALU.mult, op1=ALU.add).then_inc(tok_ready, 1)
                        continue
                    for g in range(NGR - 1):
                        for n in range(8):
                            if s == ROUTE_AT[g][n]:
                                route_step(l, g, n)

            def route_step(l, g, n):
                sl = slice(GROUPS[g][0], GROUPS[g][-1] + 1)
                base = ROUTE0_STEPS + ROUTE_STEPS * l
                c = NGR * l + g + 2
                if n < 4:
                    best(n, sl, base, NS * l + GROUPS[g][-1] + 2, c)
                elif n == 4:
                    weights(sl, base, c, xg)
                else:
                    places(n - 5, sl, base, (NGR - 1) * l + g + 1, c)
                    if n == 5 and g < NGR - 1:
                        by_expert = chosen[:, sl, :].rearrange("p j e -> p e j")
                        step(V.tensor_reduce(part[:, :], by_expert, AX_X, ALU.add), base)
                        step(V.tensor_copy(earlier[:, :], part[:, :]) if g == 0 else
                             V.tensor_tensor(earlier[:, :], earlier[:, :], part[:, :], ALU.add), base)

            all_ = slice(0, NT)
            dve.wait_ge(filled, 1)
            dve.wait_ge(consts, 13)
            for n in range(4):
                best(n, all_, 0, 1, 1, experts_=NT)
            dve.wait_ge(numbered, 1)
            weights(all_, 0, 1, xn)
            finish(all_, 0, 1, 0, all_real=True)
            assert count[0] == ROUTE0_STEPS, count[0]
            with dve.Fori(0, L - 1) as l:
                count[0] = 0
                experts(l)
                for n in range(5):
                    route_step(l, NGR - 1, n)
                finish(slice(GROUPS[-1][0], NS), ROUTE0_STEPS + ROUTE_STEPS * l, NGR * l + NGR + 1, l + 1)
                assert count[0] == ROUTE_STEPS, count[0]
            experts(L - 1, final=True)

            for b in range(B):
                k = 2 * B + 1 + b
                tiles = range(TPB * b, TPB * b + TPB)
                dve.wait_ge(got_loaded[b], 16)
                variance(k, lambda t: got[:, t, :], tiles)
                inverse(k, tiles)
                for t in tiles:
                    last = nc.vector.tensor_scalar(got[:, t, :], got[:, t, :], meanvar[:, t, 0:1], rstd[:, t:t + 1],
                                                   ALU.subtract, ALU.mult)
                last.then_inc(ln_out, 1)
                dve.wait_ge(ln_out, 2 * B + b + 1)
                sl = slice(TPB * b, TPB * b + TPB)
                nc.vector.tensor_tensor(got[:, sl, :], got[:, sl, :], x_sb[:, sl, :], ALU.add).then_inc(fin_ready, 1)


_INS = ["L0_attn_x", "L0_attn_q_w", "L0_attn_q_b", "L0_attn_k_w", "L0_attn_k_b", "L0_attn_v_w", "L0_attn_v_b",
        "L0_attn_l_w", "L0_attn_l_b", "L0_ffn_routers", "L0_ffn_W1", "L0_ffn_W2"]


def kernel(**inputs):
    import numpy as np
    import concourse.bacc as bacc
    from concourse.bass_utils import run_bass_kernel_spmd

    nc = bacc.Bacc("TRN2", target_bir_lowering=False, num_devices=1)
    arrays, args = {}, []
    for name in _INS:
        a = np.ascontiguousarray(inputs[name])
        arrays[f"in_{name}"] = a
        args.append(nc.dram_tensor(f"in_{name}", a.shape, mybir.dt.from_np(a.dtype), kind="ExternalInput").ap())
    x = arrays["in_L0_attn_x"]
    args.append(nc.dram_tensor("out", x.shape, F32, kind="ExternalOutput").ap())
    sandwich_kernel(nc, *args)
    r = run_bass_kernel_spmd(nc, [arrays], core_ids=[0])
    return r.results[0]["out"]
```

```python
from contextlib import ExitStack

import concourse.bass as bass
from concourse import mybir

F32 = mybir.dt.float32
F16 = mybir.dt.float16
BF16 = mybir.dt.bfloat16
F32R = mybir.dt.float32r
I32 = mybir.dt.int32
ALU = mybir.AluOpType
ACT = mybir.ActivationFunctionType
AX_X = mybir.AxisListType.X

P = 128
LN_EPS = 1e-5
W_SCALE = 64.0
ROUND = 1.5 * 2.0 ** 23
ROW = P + 2
INVALID = 100.0


def sandwich_kernel(nc, x_in, q_w, q_b, k_w, k_b, v_w, v_b, l_w, l_b, routers, W1, W2, out):
    B, S, D = x_in.shape
    H, DH, _ = q_w.shape
    L, _, E = routers.shape
    FF = W1.shape[2]
    NT = B * S // P
    TPB = S // P
    HD = H * DH
    NPAIR = H // 2
    NP = B * NPAIR
    FC = FF // P
    NS = NT + E - 1
    GROUPS = [range(g, min(g + 8, NS)) for g in range(0, NS, 8)]
    NGR = len(GROUPS)
    GROUPS0 = [range(0, NT - TPB), range(NT - TPB, NT)]
    NGR0 = len(GROUPS0)
    HALF = 2048
    assert D == P and DH == 64 and S == 512 and (NS + 1) * E == 512 and FF == 512 and NP // 2 == E and NS * P < 2 * HALF and HALF % P == 0

    x_rows = x_in.rearrange("b (t p) d -> p (b t) d", p=P)
    out_rows = out.rearrange("b (t p) d -> p (b t) d", p=P)
    rows = nc.dram_tensor("rows", [1 + NS * P, ROW], F32, kind="Internal").ap()
    ffn_out = nc.dram_tensor("ffn_out", [NT * P, ROW], F32, kind="Internal").ap()

    with ExitStack() as ctx:
        def sem(name):
            return ctx.enter_context(nc.semaphore(name))

        def sb(name, shape, dt=F32, of=ctx):
            return of.enter_context(nc.sbuf_tensor(name, shape, dt))

        ident = sb("ident", [P, P])
        eps = sb("eps", [P, 1])
        first_sqrt = sb("first_sqrt", [P, 1])
        tok_mem = sb("tok_mem", [P, NT * (D + ROW)])
        x_sb = tok_mem[:, 0:NT * D].rearrange("p (t d) -> p t d", d=D)
        xn = tok_mem[:, NT * D:].rearrange("p (t d) -> p t d", d=ROW)
        stats = sb("stats", [P, NT, 6])
        meanvar = sb("meanvar", [P, NT, 2])
        std = sb("std", [P, NT])
        rstd = sb("rstd", [P, NT])
        shift = sb("shift", [P, NT])
        slot_stats = sb("slot_stats", [P, 2, 6])
        w1_raw = sb("w1_raw", [P, E * FF])
        w2_sb = sb("w2_sb", [P, E * FC * D])
        router_sb = sb("router_sb", [P, L * E])
        before = sb("before", [P, P], BF16)
        ones = sb("ones", [P, P], BF16)
        iota_b = sb("iota_b", [P, P], F16)
        iota_a = sb("iota_a", [P, NS])
        label = sb("label", [P, NS])
        one_row = sb("one_row", [P, E])

        att = ctx.enter_context(ExitStack())
        xT_hi = sb("xT_hi", [P, NT * P], F16, att)
        xT_lo = sb("xT_lo", [P, NT * P], F16, att)
        wT_hi = sb("wT_hi", [P, 3, HD], F16, att)
        wT_lo = sb("wT_lo", [P, 3, HD], F16, att)
        lwT = sb("lwT", [P, NPAIR, D], F32, att)
        brow = sb("brow", [2 * NPAIR, P], F32, att)
        bcol = sb("bcol", [P, 2 * NPAIR], F32, att)
        lb_row = sb("lb_row", [1, D], F32, att)
        lb_parts = sb("lb_parts", [1, 2, D], F32R, att)
        ones_row = sb("ones_row", [1, P], F32R, att)
        vb_all = sb("vb_all", [P, HD], F32, att)
        q_pair = sb("q_pair", [P, 2, 2, S], F16, att)
        k_pair = sb("k_pair", [P, 2, 2, S], F16, att)
        q_stack = sb("q_stack", [P, 2, 2, S], F16, att)
        k_stack = sb("k_stack", [P, 2, 2, 2, S], F16, att)
        v_sb = sb("v_sb", [P, 2, TPB, P], F32, att)
        vp = sb("vp", [P, TPB, P], F32, att)
        e_sb = tok_mem[:, 0:TPB * 2 * S].rearrange("p (t h s) -> p t h s", t=TPB, h=2)
        ctxT = sb("ctxT", [P, NPAIR, B * S], F32, att)
        w_raw = ctxT[:, 0:2, :].rearrange("p a (b j c) -> p (a b) j c", b=2, j=NPAIR)
        mx = sb("mx", [P, TPB, 2], F32, att)
        nmx = sb("nmx", [P, TPB, 2], F32, att)
        minus_sc = sb("minus_sc", [P, 1], F32, att)
        esum = sb("esum", [P, TPB, 2], F32, att)
        rsum = sb("rsum", [P, TPB, 2], F32, att)
        att_n = xn
        att.close()

        hT = sb("hT", [P, 2, FC, P])
        w1_hi = sb("w1_hi", [P, E * FF], F32R)
        w1_lo = sb("w1_lo", [P, E * FF], F32R)
        expert_m = sb("expert_m", [P, NS, E])
        xg = sb("xg", [P, NS, ROW])
        on_b = sb("on_b", [P, NS, P], F16)
        on_a = sb("on_a", [P, NS, NS], F16)
        lg = sb("lg", [P, NS, E])
        rel = sb("rel", [P, NS, E])
        cand = sb("cand", [P, NS, E])
        ex = sb("ex", [P, NS, E])
        chosen = sb("chosen", [P, NS, E], BF16)
        part = sb("part", [P, E])
        earlier = sb("earlier", [P, E], BF16)
        ranked = sb("ranked", [P, NS, E])
        first = sb("first", [P, NS, E])
        under = sb("under", [P, NS, E])
        lmax = sb("lmax", [P, NS])
        zsum = sb("zsum", [P, NS])
        weight = sb("weight", [P, NS])
        expert = sb("expert", [P, NS])
        empty = sb("empty", [P, NS])
        rank = sb("rank", [P, NS])
        tile_in = sb("tile_in", [P, NS])
        pos_a = sb("pos_a", [P, NS])
        pos_b = sb("pos_b", [P, NS])
        tiles_e = sb("tiles_e", [P, E])
        cum_e = sb("cum_e", [P, E])
        first_e = sb("first_e", [P, E])
        eid = sb("eid", [P, NS])
        beyond = sb("beyond", [P, NS])
        w_off = sb("w_off", [P, NS], I32)
        src_i = sb("src_i", [P, NS], I32)
        slot_hi = sb("slot_hi", [P, 2, P], F32R)
        slot_lo = sb("slot_lo", [P, 2, P], F32R)
        th = sb("th", [P, 2, FF])
        act_h = sb("act_h", [P, 2, FF])
        yT = sb("yT", [P, 2, P])
        tok_i = sb("tok_i", [P, NS], I32)
        rowsT = hT[:, :, :, :].rearrange("p u c k -> p u (c k)")
        got = w1_raw[:, 0:NT * ROW].rearrange("p (t d) -> p t d", d=ROW)

        ps = [ctx.enter_context(nc.psum_tensor(f"ps{i}", [P, 512], F32)) for i in range(8)]
        ps_ctx, ps_q, ps_k, ps_v = ps[4:8]

        x_loaded = [sem(f"x_loaded{b}") for b in range(B)]
        b_loaded, w_loaded, vb_loaded, ffn_loaded = sem("b_loaded"), sem("w_loaded"), sem("vb_loaded"), sem("ffn_loaded")
        router_loaded = sem("router_loaded")
        consts = sem("consts")
        ln_stat, ln_var, ln_std, ln_rstd, ln_out = sem("ln_stat"), sem("ln_var"), sem("ln_std"), sem("ln_rstd"), sem("ln_out")
        lb_hi = sem("lb_hi")
        ln_out_s = sem("ln_out_s")
        prep_T, prep_hi, prep_done = sem("prep_T"), sem("prep_hi"), sem("prep_done")
        q_ready, k_ready, v_ready = sem("q_ready"), sem("k_ready"), sem("v_ready")
        q_hi, k_hi, q_lo, k_lo = sem("q_hi"), sem("k_hi"), sem("q_lo"), sem("k_lo")
        v_out = sem("v_out")
        q_stacked, k_stacked = ([[sem(f"{m}_stacked{u}{hd}") for hd in range(2)] for u in range(2)]
                                for m in "qk")
        scores_ready, max_done, nmax_done, exp_done = sem("scores_ready"), sem("max_done"), sem("nmax_done"), sem("exp_done")
        rsum_done, vp_done, ctx_step, ctx_copied = sem("rsum_done"), sem("vp_done"), sem("ctx_step"), sem("ctx_copied")
        proj_ready, shift_ready, att_done, x1_done = sem("proj_ready"), sem("shift_ready"), sem("att_done"), sem("x1_done")
        xn_T, xn_copied, rows_written = sem("xn_T"), sem("xn_copied"), sem("rows_written")
        numbered, filled = sem("numbered"), sem("filled")
        logits0_ready, lg_copied, rel_ready, exp_ready = sem("logits0_ready"), sem("lg_copied"), sem("rel_ready"), sem("exp_ready")
        chosen_ready, ranks_ready, ranks_read = sem("chosen_ready"), sem("ranks_ready"), sem("ranks_read")
        weight_ready, on_a_ready, on_b_ready, inv_ready = sem("weight_ready"), sem("on_a_ready"), sem("on_b_ready"), sem("inv_ready")
        src_ready, w_off_ready = sem("src_ready"), sem("w_off_ready")
        route = sem("route")
        gathered = [sem(f"gathered{t}") for t in range(NS)]
        w1_hi_ready, w1_lo_pool, w1_lo_dve, lo_out = sem("w1_hi_ready"), sem("w1_lo_pool"), sem("w1_lo_dve"), sem("lo_out")
        xT_in, xT_out, h_in, th_done, h_done = sem("xT_in"), sem("xT_out"), sem("h_in"), sem("th_done"), sem("h_done")
        hT_in, hT_out, y_in, y_done = sem("hT_in"), sem("hT_out"), sem("y_in"), sem("y_done")
        yT_in, yT_out, logit_in = sem("yT_in"), sem("yT_out"), sem("logit_in")
        y_written = sem("y_written")
        slot_stat, slot_done = sem("slot_stat"), sem("slot_done")
        scattered = sem("scattered")
        got_loaded = [sem(f"got_loaded{b}") for b in range(B)]
        fin_std, fin_rstd, fin_shift = sem("fin_std"), sem("fin_rstd"), sem("fin_shift")
        fin_norm = [sem("fin_norm_v"), sem("fin_norm_s")]
        fin_ready, stored = sem("fin_ready"), sem("stored")
        block = ctx.enter_context(nc.Block())

        ps_xT, ps_yT, ps_y, ps_rank = ps[0:4]
        ps_h, ps_hT, ps_inv = ps[4:6], ps[6:8], ps[0]
        ROUTE0_STEPS, ROUTE_STEPS = 33, 65
        ROUTE_AT = [[tiles[-1] + 5 + n for n in range(8)] for tiles in GROUPS[:-1]]
        last_group = GROUPS[-2][-1] + 5
        ROUTE_AT[-1] = [last_group + n for n in (0, 0, 1, 1, 2, 3, 4, 5)]
        RANKS_AT = [at[3] for at in ROUTE_AT]
        EXP_AT = [at[0] for at in ROUTE_AT]
        ps_out = [ps_q, ps_k, ps_v, ps_ctx]
        ps_lg = [ps[1]] * (B - 1) + [ps[0]]
        EARLY_SPLITS, DVE_SPLITS = 4, 5
        NV = 2
        SC = float(DH) ** -0.5 / (W_SCALE * W_SCALE)
        PREP = [("x", b, 0) for b in range(B)] + [("w", m, g) for m in (1, 0, 2, 3) for g in range(2)]
        NPREP = len(PREP) - 2

        @block.sync
        def _(sp):
            for b in range(B):
                sp.dma_start(x_sb[:, b * TPB:(b + 1) * TPB, :], x_rows[:, b * TPB:(b + 1) * TPB, :]).then_inc(x_loaded[b], 16)

            def stack_k(u):
                for hd in range(2):
                    for half in range(2):
                        sp.dma_start(k_stack[64 * half:64 * half + 64, u, hd, :, :],
                                     k_pair[64 * hd:64 * hd + 64, u, :, :]).then_inc(k_stacked[u][hd], 16)

            def stack_q(u):
                for half, hd, hl in ((0, 0, 0), (1, 0, 1), (1, 1, 0), (0, 1, 1)):
                    sp.dma_start(q_stack[64 * half:64 * half + 64, u, hd, :],
                                 q_pair[64 * hd:64 * hd + 64, u, hl, :]).then_inc(q_stacked[u][hd], 16)

            def load_expert(e):
                sp.dma_start(w1_raw[:, bass.ds(e * FF, FF)].unsqueeze(1),
                             W1[bass.ds(e, 1), :, :].rearrange("e d f -> d e f")).then_inc(ffn_loaded, 16)
                sp.dma_start(w2_sb[:, bass.ds(e * FC * D, FC * D)].rearrange("p (c d) -> p c d", c=FC),
                             W2[bass.ds(e, 1), :, :].rearrange("e (c p) d -> p (e c) d", p=P)).then_inc(ffn_loaded, 16)

            for i in range(2):
                sp.wait_ge(k_lo, i + 1)
                stack_k(i)
                sp.wait_ge(q_lo, i + 1)
                stack_q(i)
            load_expert(0)
            with sp.Fori(1, NP // 2) as g:
                scored = [sp.to_reg(16 * g - 8), sp.to_reg(16 * g)]
                written = [sp.to_reg(2 * g + 1), sp.to_reg(2 * g + 2)]
                for u in range(2):
                    sp.wait_ge(scores_ready, scored[u])
                    sp.wait_ge(k_lo, written[u])
                    stack_k(u)
                    sp.wait_ge(q_lo, written[u])
                    stack_q(u)
                load_expert(g)
            sp.wait_ge(ctx_step, 4 * NP)
            for b in range(B):
                sp.dma_start(x_sb[:, b * TPB:(b + 1) * TPB, :], x_rows[:, b * TPB:(b + 1) * TPB, :]).then_inc(x_loaded[b], 16)
            sp.wait_ge(ffn_loaded, 32 * E)
            sp.dma_start(rows[0:1, :], w1_raw[0:1, 0:ROW]).then_inc(rows_written, 16)
            sp.dma_start(rows[1 + NT * P:1 + NS * P, :].rearrange("(t p) d -> p t d", p=P),
                         w1_raw[:, 0:(NS - NT) * ROW].rearrange("p (t d) -> p t d", d=ROW)).then_inc(rows_written, 16)
            sp.wait_ge(numbered, 1)
            sp.wait_ge(weight_ready, NGR0)
            for b in range(B):
                sp.dma_start(rows[1 + b * S:1 + (b + 1) * S, :].rearrange("(t p) d -> p t d", p=P),
                             xn[:, b * TPB:(b + 1) * TPB, :]).then_inc(rows_written, 16)

            with sp.Fori(0, L - 1) as l:
                weighted = [sp.to_reg(NGR * l + g + NGR0 + 1) for g in range(NGR)]
                sp.wait_ge(xT_in, sp.to_reg(NS * l + NS))
                for g, tiles in enumerate(GROUPS):
                    sp.wait_ge(weight_ready, weighted[g])
                    lo, hi = tiles[0], tiles[-1] + 1
                    sp.dma_start(rows[1 + lo * P:1 + hi * P, :].rearrange("(t p) d -> p t d", p=P),
                                 xg[:, lo:hi, :]).then_inc(y_written, 16)

            sp.wait_ge(scattered, 16 * NS)
            for b in range(B):
                sp.dma_start(got[:, b * TPB:(b + 1) * TPB, :],
                             ffn_out[b * S:(b + 1) * S, :].rearrange("(t p) d -> p t d", p=P)).then_inc(got_loaded[b], 16)
            for b in range(B):
                sp.wait_ge(fin_ready, b + 1)
                sp.dma_start(out_rows[:, b * TPB:(b + 1) * TPB, :], got[:, b * TPB:(b + 1) * TPB, 0:D]).then_inc(stored, 16)
            sp.wait_ge(stored, 16 * B)

        @block.gpsimd
        def _(pool):
            nc.gpsimd.memset(ident[:, :], 0.0).then_inc(consts, 1)
            nc.gpsimd.memset(eps[:, :], LN_EPS).then_inc(consts, 1)
            pool.wait_ge(consts, 2)
            nc.gpsimd.affine_select(out=ident[:, :], in_=ident[:, :], compare_op=ALU.not_equal, fill=1.0,
                                    base=0, pattern=[[-1, P]], channel_multiplier=1).then_inc(consts, 1)
            nc.gpsimd.memset(minus_sc[:, :], -SC).then_inc(consts, 1)
            g = dict(allow_small_or_imprecise_dtypes=True)
            nc.gpsimd.iota(iota_b[:, :], [[1, P]], base=0, channel_multiplier=0, **g).then_inc(consts, 1)
            nc.gpsimd.iota(iota_a[:, :], [[1, NS]], base=0, channel_multiplier=0, **g).then_inc(consts, 1)
            low_tiles = HALF // P
            nc.gpsimd.iota(label[:, 0:low_tiles], [[P, low_tiles]], base=1, channel_multiplier=1, **g).then_inc(consts, 1)
            nc.gpsimd.iota(label[:, low_tiles:NS], [[P, NS - low_tiles]], base=1 - HALF, channel_multiplier=1, **g).then_inc(consts, 1)
            nc.gpsimd.memset(one_row[:, :], 1.0).then_inc(consts, 1)
            nc.gpsimd.memset(ones[:, :], 1.0).then_inc(consts, 1)
            nc.gpsimd.memset(before[:, :], 1.0).then_inc(consts, 1)
            pool.wait_ge(consts, 11)
            nc.gpsimd.affine_select(out=before[:, :], in_=before[:, :], compare_op=ALU.is_ge, fill=0.0,
                                    base=-1, pattern=[[1, P]], channel_multiplier=-1).then_inc(consts, 1)
            pool.dma_start(router_sb[:, :].rearrange("p (l e) -> p l e", l=L),
                           routers.rearrange("l d e -> d l e")).then_inc(router_loaded, 16)
            with pool.Fori(0, NP) as i:
                for n in range(2 * TPB):
                    pool.wait_ge(max_done, 8 * i + (n + 1))
                    nc.gpsimd.tensor_tensor(nmx[:, n // 2, n % 2:n % 2 + 1], mx[:, n // 2, n % 2:n % 2 + 1],
                                            minus_sc[:, :], ALU.mult).then_inc(nmax_done, 1)

            pool.wait_ge(ctx_step, 4 * NP)
            nc.gpsimd.iota(xn[:, :, D:ROW], [[P, NT], [0, ROW - D]], base=0, channel_multiplier=1,
                           allow_small_or_imprecise_dtypes=True).then_inc(numbered, 1)
            pool.wait_ge(proj_ready, B)
            nc.gpsimd.iota(expert_m[:, :, :], [[0, NS], [1, E]], base=-E, channel_multiplier=0,
                           allow_small_or_imprecise_dtypes=True).then_inc(filled, 1)

            def gather(t):
                pool.indirect_dma_start(xg[:, t, :], None, rows, bass.IndirectOffsetOnAxis(ap=src_i[:, t:t + 1], axis=0)
                                        ).then_inc(gathered[t], 16)

            for e in range(E - DVE_SPLITS):
                pool.wait_ge(w1_hi_ready, e + 1)
                nc.gpsimd.tensor_tensor(w1_lo[:, e * FF:(e + 1) * FF], w1_raw[:, e * FF:(e + 1) * FF],
                                        w1_hi[:, e * FF:(e + 1) * FF], ALU.subtract).then_inc(w1_lo_pool, 1)
            pool.wait_ge(rows_written, 16 * (B + 2))
            pool.wait_ge(src_ready, 1)
            for t in range(NS):
                gather(t)
            with pool.Fori(0, L - 2) as l:
                pool.wait_ge(y_written, 16 * NGR * l + 16 * NGR)
                pool.wait_ge(src_ready, l + 2)
                all_in = pool.to_reg(16 * l + 32)
                for t in range(NS):
                    gather(t)
                pool.wait_ge(gathered[NS - 1], all_in)
            pool.wait_ge(y_written, 16 * NGR * (L - 1))
            pool.wait_ge(src_ready, L)
            for t in range(NS):
                gather(t)
            for t in range(NS):
                pool.wait_ge(slot_done, t + 1)
                pool.indirect_dma_start(ffn_out, bass.IndirectOffsetOnAxis(ap=tok_i[:, t:t + 1], axis=0),
                                        xg[:, t, :], None, bounds_check=NT * P - 1, oob_is_err=False
                                        ).then_inc(scattered, 16)

        @block.tensor
        def _(pe):
            pe.wait_ge(consts, 3)
            pe.wait_ge(b_loaded, 48)
            nb = 2 * NPAIR
            nc.tensor.transpose(ps_v[:, 0:nb], brow[:, :], ident[0:nb, 0:nb]).then_inc(prep_T, 1)
            def prepare(n):
                kind, m, g = PREP[n]
                if n >= 4:
                    pe.wait_ge(prep_done, n - 3 + 1)
                if n == B:
                    pe.wait_ge(w_loaded, 16 * 4)
                if kind == "x":
                    if m < NV:
                        pe.wait_ge(ln_out, m + 1)
                    else:
                        pe.wait_ge(ln_out_s, m - NV + 1)
                for c in range(4):
                    src_ = w_raw[:, m, 4 * g + c, :] if kind == "w" else xn[:, TPB * m + c, 0:D]
                    last = nc.tensor.transpose(ps[n % 4][:, c * P:(c + 1) * P], src_, ident[:, :])
                last.then_inc(prep_T, 1)

            for n in range(NPREP):
                prepare(n)

            PASSES = [(wT_hi, xT_hi), (wT_lo, xT_hi), (wT_hi, xT_lo)]

            def project_qk(dst, m, tok, pair):
                for n, (w, x) in enumerate(PASSES):
                    last = nc.tensor.matmul(dst[:, :], w[:, m, bass.ds(pair * P, P)], x[:, bass.ds(tok, S)],
                                            start=(n == 0), stop=(n == 2))
                return last

            def project_v(tok, pair):
                for t in range(TPB):
                    for n, (w, x) in enumerate(PASSES):
                        last = nc.tensor.matmul(ps_v[:, t * P:(t + 1) * P], x[:, bass.ds(tok + t * P, P)],
                                                w[:, 2, bass.ds(pair * P, P)], start=(n == 0), stop=(n == 2))
                return last

            def scores(i, u, kt, first):
                for hd in range(2):
                    n = 2 * kt + hd
                    if kt == 0:
                        pe.wait_ge(q_stacked[u][hd], 16 * i + (32 - 16 * u))
                        pe.wait_ge(k_stacked[u][hd], 16 * i + (32 - 16 * u))
                    if not (first and n < 4):
                        pe.wait_ge(exp_done, 8 * i + (n - 3))
                    for hl in range(2):
                        last = nc.tensor.matmul(ps[n % 4][:, :], k_stack[:, u, hd, hl, kt * P:(kt + 1) * P],
                                                q_stack[:, u, hd, :], start=(hl == 0), stop=(hl == 1))
                    last.then_inc(scores_ready, 1)

            def context(i, kt, first=False):
                if kt == 0 and not first:
                    pe.wait_ge(ctx_copied, i)
                pe.wait_ge(vp_done, 4 * i + (kt + 1))
                for hd in range(2):
                    last = nc.tensor.matmul(ps_ctx[64 * hd:64 * hd + 64, :], vp[:, kt, 64 * hd:64 * hd + 64],
                                            e_sb[:, kt, hd, :], start=(kt == 0), stop=(kt == TPB - 1))
                last.then_inc(ctx_step, 1)

            def pair_step(i, u, first=False, second=False, ahead=2):
                for kt in range(TPB):
                    scores(i, u, kt, first)
                    if ahead >= 1 and kt == 2:
                        pe.wait_ge(v_out, i + 1)
                        project_v(((i + 1) // NPAIR) * S, (i + 1) % NPAIR).then_inc(v_ready, 1)
                    if ahead >= 2 and kt == 0:
                        pe.wait_ge(k_lo, i + 2)
                        project_qk(ps_k, 1, ((i + 2) // NPAIR) * S, (i + 2) % NPAIR).then_inc(k_ready, 1)
                    if ahead >= 2 and kt == 1:
                        pe.wait_ge(q_lo, i + 2)
                        project_qk(ps_q, 0, ((i + 2) // NPAIR) * S, (i + 2) % NPAIR).then_inc(q_ready, 1)
                    if not first:
                        context(i - 1, kt, first=second)

            pe.wait_ge(prep_done, B + 2 + 1)
            project_qk(ps_k, 1, 0, 0).then_inc(k_ready, 1)
            pe.wait_ge(prep_done, B + 4 + 1)
            project_qk(ps_q, 0, 0, 0).then_inc(q_ready, 1)
            pe.wait_ge(prep_done, NPREP + 1)
            project_v(0, 0).then_inc(v_ready, 1)
            pe.wait_ge(k_lo, 1)
            project_qk(ps_k, 1, 0, 1).then_inc(k_ready, 1)
            pe.wait_ge(q_lo, 1)
            project_qk(ps_q, 0, 0, 1).then_inc(q_ready, 1)
            for n in range(NPREP, len(PREP)):
                prepare(n)
            pe.wait_ge(prep_done, len(PREP) + 1)
            pair_step(0, 0, first=True)
            pair_step(1, 1, second=True)
            with pe.Fori(1, NP // 2 - 1) as g:
                for u in range(2):
                    pair_step(2 * g + u, u)
            pair_step(NP - 2, 0, ahead=1)
            pair_step(NP - 1, 1, ahead=0)

            def project_out(b):
                pe.wait_ge(ctx_copied, NPAIR * (b + 1))
                for n in range(2):
                    nc.tensor.matmul(ps_out[b][:, :].rearrange("p (c d) -> p c d", d=D), ones_row[:, :],
                                     lb_parts[:, n, :].unsqueeze(1).broadcast_to([1, TPB, D]), start=(n == 0), stop=False)
                for c in range(TPB):
                    for j in range(NPAIR):
                        last = nc.tensor.matmul(ps_out[b][:, c * D:(c + 1) * D], ctxT[:, j, b * S + c * P:b * S + (c + 1) * P],
                                                lwT[:, j, :], start=False, stop=(j == NPAIR - 1 and c == TPB - 1))
                last.then_inc(proj_ready, 1)

            def logits(b):
                pe.wait_ge(ln_out, NV + b + 1)
                for c in range(TPB):
                    last = nc.tensor.transpose(ps[2][:, c * P:(c + 1) * P], xn[:, b * TPB + c, 0:D], ident[:, :])
                last.then_inc(xn_T, 1)
                pe.wait_ge(xn_copied, b + 1)
                for c in range(TPB):
                    j = b * TPB + c
                    last = nc.tensor.matmul(ps_lg[b][:, j * E:(j + 1) * E], rowsT[:, b % 2, c * P:(c + 1) * P],
                                            router_sb[:, 0:E], start=True, stop=True)
                return last

            project_out(0)
            for kt in range(TPB):
                context(NP - 1, kt)
            pe.wait_ge(ffn_loaded, 32 * E)
            pe.wait_ge(router_loaded, 16)
            for b in range(1, B):
                project_out(b)
                if b >= 2:
                    logits(b - 2)
            logits(B - 2).then_inc(logits0_ready, 1)
            logits(B - 1).then_inc(logits0_ready, 1)

            def count_ranks(tiles, carry, total):
                end = NS * E + E if total else (tiles[-1] + 1) * E
                by_tile = lambda j: ps_rank[:, j * E:end].rearrange("p (j e) -> p j e", e=E)
                bcast = lambda a, j: a.unsqueeze(1).broadcast_to([P, end // E - j, E])
                if carry:
                    nc.tensor.matmul(by_tile(tiles[0]), ones[:, :], bcast(earlier[:, :], tiles[0]), start=True, stop=False)
                for j in tiles:
                    last = nc.tensor.matmul(ps_rank[:, j * E:(j + 1) * E], before[:, :], chosen[:, j, :],
                                            start=(j == tiles[0] and not carry), stop=(j == tiles[-1] and not total))
                    if (j + 1) * E < end:
                        last = nc.tensor.matmul(by_tile(j + 1), ones[:, :], bcast(chosen[:, j, :], j + 1),
                                                start=False, stop=(j == tiles[-1]))
                return last

            def invert(tiles, count, last_group):
                half = len(tiles) // 2
                for j in tiles:
                    if j in (0, half):
                        pe.wait_ge(on_a_ready, 2 * count - (j == 0))
                    if j == last_group:
                        pe.wait_ge(on_b_ready, count)
                    last = nc.tensor.matmul(ps_inv[:, 0:NS], on_b[:, j, :], on_a[:, j, :], start=(j == 0), stop=(j == tiles[-1]))
                last.then_inc(inv_ready, 1)

            for g in range(NGR0):
                pe.wait_ge(chosen_ready, g + 1)
                if g > 0:
                    pe.wait_ge(ranks_read, g)
                count_ranks(GROUPS0[g], g > 0, g == NGR0 - 1).then_inc(ranks_ready, 1)
            invert(range(NT), 1, GROUPS0[-1][0])

            OG = 8
            offs = [pe.alloc_register(f"w_off{t}") for t in range(2 * OG)]

            def experts(l, final=False):
                base = l * NS
                pe.wait_ge(w_off_ready, l + 1)
                first_in = pe.to_reg(16 * l + 16)
                off = {}
                for s in range(-1, NS + (2 if final else 4)):
                    if (s + 1) % OG == 0 and s + 1 < NS:
                        lo, hi = s + 1, min(s + 1 + OG, NS)
                        half = (lo // OG) % 2 * OG
                        pe.load(offs[half:half + hi - lo], w_off[0:1, lo:hi])
                        for t in range(lo, hi):
                            off[t] = pe.snap(offs[half + t - lo], min_val=0, max_val=(E - 1) * FF)
                    t = s
                    if 0 <= t < NS:
                        pe.wait_ge(lo_out, base + (t + 1))
                        if t >= 2:
                            pe.wait_ge(h_done, base + (t - 1))
                        for n, (rows_t, w) in enumerate(((slot_hi, w1_hi), (slot_lo, w1_hi), (slot_hi, w1_lo))):
                            last = nc.tensor.matmul(ps_h[t % 2][:, :], rows_t[:, t % 2, :], w[:, bass.ds(off[t], FF)],
                                                    start=(n == 0), stop=(n == 2))
                        last.then_inc(h_in, 1)
                    t = s + 1
                    if t < NS:
                        pe.wait_ge(gathered[t], first_in if t == 0 else 16 * l + 16)
                        if t > 0:
                            pe.wait_ge(lo_out, base + t)
                        nc.tensor.transpose(ps_xT[:, 0:P], xg[:, t, 0:D], ident[:, :]).then_inc(xT_in, 1)
                    t = s - 1
                    if 0 <= t < NS:
                        pe.wait_ge(h_done, base + (t + 1))
                        if t >= 2:
                            pe.wait_ge(hT_out, base + (t - 1))
                        for c in range(FC):
                            last = nc.tensor.transpose(ps_hT[t % 2][:, c * P:(c + 1) * P],
                                                       act_h[:, t % 2, c * P:(c + 1) * P], ident[:, :])
                        last.then_inc(hT_in, 1)
                    t = s - 2
                    if 0 <= t < NS:
                        pe.wait_ge(hT_out, base + (t + 1))
                        if t > 0:
                            pe.wait_ge(y_done, base + t)
                        for c in range(FC):
                            last = nc.tensor.matmul(ps_y[:, 0:D], hT[:, t % 2, c, :],
                                                    w2_sb[:, bass.ds(off[t] + c * D, D)], start=(c == 0), stop=(c == FC - 1))
                        last.then_inc(y_in, 1)
                    if final:
                        continue
                    t = s - 4
                    if 0 <= t < NS:
                        pe.wait_ge(yT_out, base + (t + 1))
                        if t > 0:
                            pe.wait_ge(lg_copied, base + t + NGR0)
                        nc.tensor.matmul(ps_yT[:, P:P + E], yT[:, t % 2, :], router_sb[:, bass.ds((l + 1) * E, E)],
                                         start=True, stop=True).then_inc(logit_in, 1)
                    t = s - 3
                    if 0 <= t < NS:
                        pe.wait_ge(y_done, base + (t + 1))
                        nc.tensor.transpose(ps_yT[:, 0:P], xg[:, t, 0:D], ident[:, :]).then_inc(yT_in, 1)
                    for g in range(NGR - 1):
                        if s == RANKS_AT[g] + 1:
                            ranks(l, g)

            def ranks(l, g):
                pe.wait_ge(chosen_ready, NGR * l + g + NGR0 + 1)
                if g > 0:
                    pe.wait_ge(ranks_read, (NGR - 1) * l + g + NGR0 - 1)
                count_ranks(GROUPS[g], g > 0, g == NGR - 1).then_inc(ranks_ready, 1)

            pe.wait_ge(w1_lo_pool, E - DVE_SPLITS)
            pe.wait_ge(w1_lo_dve, DVE_SPLITS)
            with pe.Fori(0, L - 1) as l:
                experts(l)
                ranks(l, NGR - 1)
                invert(range(NS), l + 2, GROUPS[-1][0])
            experts(L - 1, final=True)

        @block.scalar
        def _(act):
            for m, (dst, bias) in enumerate(((0, q_b), (NPAIR, k_b))):
                act.dma_start(brow[dst:dst + NPAIR, :], bias.rearrange("(j r) o p -> j (r o p)", r=2)).then_inc(b_loaded, 16)
            act.dma_start(lb_row[:, :], l_b).then_inc(b_loaded, 16)
            for m, w in enumerate((q_w, k_w, v_w)):
                act.dma_start(w_raw[:, m], w.rearrange("(j r) p d -> (r p) j d", r=2)).then_inc(w_loaded, 16)
            act.dma_start(w_raw[:, 3], l_w.rearrange("o (j p) -> o j p", p=P)).then_inc(w_loaded, 16)
            act.dma_start(vb_all[:, :], v_b.rearrange("h o p -> o (h p)").broadcast_to([P, HD])).then_inc(vb_loaded, 16)

            act.wait_ge(consts, 2)

            def sqrt(k):
                act.wait_ge(ln_var, k + 1)
                if k == 0:
                    sl = slice(0, NT)
                else:
                    b_ = (k - 1) // 2 if k <= 2 * B else k - 2 * B - 1
                    sl = slice(TPB * b_, TPB * b_ + TPB)
                nc.scalar.activation(std[:, sl], meanvar[:, sl, 1], ACT.Sqrt, bias=eps[:, 0:1]).then_inc(ln_std, 1)

            nc.scalar.activation(first_sqrt[:, :], eps[:, :], ACT.Sqrt)
            sqrt(0)
            act.wait_ge(shift_ready, 1)
            for b in range(NV, B):
                for t in range(TPB * b, TPB * b + TPB):
                    last = nc.scalar.activation(xn[:, t, 0:D], x_sb[:, t, :], ACT.Identity, bias=shift[:, t:t + 1],
                                                scale=rstd[:, t:t + 1])
                last.then_inc(ln_out_s, 1)
            for n, (kind, m, g) in enumerate(PREP[:NPREP]):
                act.wait_ge(prep_T, n + 2)
                if kind == "w":
                    nc.scalar.activation(wT_hi[:, m, 512 * g:512 * g + 512], ps[n % 4][:, :], ACT.Copy,
                                         scale=W_SCALE).then_inc(prep_hi, 1)
                else:
                    nc.scalar.activation(xT_hi[:, S * m:S * m + S], ps[n % 4][:, :], ACT.Copy).then_inc(prep_hi, 1)

            def high(dst, u, src_, ready, done, stacked, i, col):
                act.wait_ge(ready, i + 1)
                if stacked is not None:
                    for hd in range(2):
                        act.wait_ge(stacked[u][hd], 16 * i - 16 * u)
                nc.scalar.activation(dst[:, u, 0, :], src_[:, :], ACT.Identity, bias=bcol[:, bass.ds(col, 1)]).then_inc(done, 1)

            def k_high(i, u, pair, first=False):
                high(k_pair, u, ps_k, k_ready, k_hi, None if first else k_stacked, i, pair + NPAIR)

            def q_high(i, u, pair, first=False):
                high(q_pair, u, ps_q, q_ready, q_hi, None if first else q_stacked, i, pair)

            def copy_context(i):
                act.wait_ge(ctx_step, 4 * i + 4)
                flat = ctxT[:, :, :].rearrange("p j t -> p (j t)")
                nc.scalar.activation(flat[:, bass.ds((i % NPAIR) * (B * S) + (i // NPAIR) * S, S)], ps_ctx[:, :],
                                     ACT.Copy).then_inc(ctx_copied, 1)

            def pair_step(i, u, first=False, project=True):
                for kt in range(TPB):
                    if not first:
                        act.wait_ge(ctx_step, 4 * i + (kt - 3))
                    if not first and kt == TPB - 1:
                        copy_context(i - 1)
                    for hd in range(2):
                        act.wait_ge(nmax_done, 8 * i + (2 * kt + hd + 1))
                        nc.scalar.activation(e_sb[:, kt, hd, :], ps[(2 * kt + hd) % 4][:, :], ACT.Exp,
                                             bias=nmx[:, kt, hd:hd + 1], scale=SC,
                                             accum_out=esum[:, kt, hd:hd + 1]).then_inc(exp_done, 1)
                    if project and kt == 1:
                        k_high(i + 2, u, (i + 2) % NPAIR)
                    if project and kt == 2:
                        q_high(i + 2, u, (i + 2) % NPAIR)
            act.wait_ge(b_loaded, 48)
            nc.scalar.activation(lb_parts[:, 0, :], lb_row[:, :], ACT.Copy).then_inc(lb_hi, 1)
            act.wait_ge(prep_done, 1)
            for i in range(2):
                k_high(i, i, i, first=True)
                q_high(i, i, i, first=True)
            pair_step(0, 0, first=True)
            pair_step(1, 1)
            with act.Fori(1, NP // 2 - 1) as g:
                for u in range(2):
                    pair_step(2 * g + u, u)
            pair_step(NP - 2, 0, project=False)
            pair_step(NP - 1, 1, project=False)
            copy_context(NP - 1)

            def copy_rows(b):
                act.wait_ge(xn_T, b + 1)
                nc.scalar.activation(rowsT[:, b % 2, :], ps[2][:, :], ACT.Copy).then_inc(xn_copied, 1)

            def normalise(b):
                sqrt(2 * b + 1)
                act.wait_ge(shift_ready, b + 2)
                for t in range(TPB * b, TPB * b + TPB):
                    last = nc.scalar.activation(att_n[:, t, 0:D], ps_out[b][:, (t % TPB) * D:(t % TPB + 1) * D], ACT.Identity,
                                                bias=shift[:, t:t + 1], scale=rstd[:, t:t + 1])
                last.then_inc(att_done, 1)
                if b == B - 1:
                    copy_rows(b - 1)
                sqrt(2 * b + 2)

            normalise(0)
            for b in range(1, B):
                normalise(b)
                if b < B - 1:
                    copy_rows(b - 1)

            def exponentials(tiles, count):
                act.wait_ge(rel_ready, count)
                sl = slice(tiles[0], tiles[-1] + 1)
                nc.scalar.activation(ex[:, sl, :], rel[:, sl, :], ACT.Exp).then_inc(exp_ready, 1)

            def split_high(e):
                nc.scalar.activation(w1_hi[:, e * FF:(e + 1) * FF], w1_raw[:, e * FF:(e + 1) * FF], ACT.Copy
                                     ).then_inc(w1_hi_ready, 1)

            act.wait_ge(ffn_loaded, 32 * E)
            for e in range(EARLY_SPLITS):
                split_high(e)
            for g, tiles in enumerate(GROUPS0):
                if g == NGR0 - 1:
                    copy_rows(B - 1)
                act.wait_ge(logits0_ready, g + 1)
                sl = slice(tiles[0], tiles[-1] + 1)
                nc.scalar.activation(lg[:, sl, :].rearrange("p j e -> p (j e)"), ps_lg[-1 if g else 0][:, sl.start * E:sl.stop * E],
                                     ACT.Copy).then_inc(lg_copied, 1)
            for g, tiles in enumerate(GROUPS0):
                exponentials(tiles, g + 1)
            for e in range(EARLY_SPLITS, E):
                split_high(e)

            def experts(l, final=False):
                base = l * NS
                for s in range(-1, NS + (2 if final else 4)):
                    t = s
                    if 0 <= t < NS:
                        act.wait_ge(h_in, base + (t + 1))
                        if t >= 2:
                            act.wait_ge(h_done, base + (t - 1))
                        nc.scalar.activation(th[:, t % 2, :], ps_h[t % 2][:, :], ACT.Tanh, scale=0.5).then_inc(th_done, 1)
                    t = s + 1
                    if t < NS:
                        act.wait_ge(xT_in, base + (t + 1))
                        if t >= 2:
                            act.wait_ge(h_in, base + (t - 1))
                        nc.scalar.activation(slot_hi[:, t % 2, :], ps_xT[:, 0:P], ACT.Copy).then_inc(xT_out, 1)
                    t = s - 1
                    if 0 <= t < NS:
                        act.wait_ge(hT_in, base + (t + 1))
                        if t >= 2:
                            act.wait_ge(y_in, base + (t - 1))
                        nc.scalar.activation(hT[:, t % 2, :, :].rearrange("p c k -> p (c k)"), ps_hT[t % 2][:, :],
                                             ACT.Copy).then_inc(hT_out, 1)
                    t = s - 2
                    if 0 <= t < NS:
                        act.wait_ge(y_in, base + (t + 1))
                        nc.scalar.activation(xg[:, t, 0:D], ps_y[:, 0:D], ACT.Copy,
                                             scale=xg[:, t, D + 1:D + 2]).then_inc(y_done, 1)
                    if final:
                        continue
                    t = s - 3
                    if 0 <= t < NS:
                        act.wait_ge(yT_in, base + (t + 1))
                        if t >= 2:
                            act.wait_ge(logit_in, base + (t - 1))
                        nc.scalar.activation(yT[:, t % 2, :], ps_yT[:, 0:P], ACT.Copy).then_inc(yT_out, 1)
                    t = s - 4
                    if 0 <= t < NS:
                        act.wait_ge(logit_in, base + (t + 1))
                        nc.scalar.activation(lg[:, t, :], ps_yT[:, P:P + E], ACT.Copy).then_inc(lg_copied, 1)
                    for g in range(NGR - 1):
                        if s == EXP_AT[g] + 1:
                            exponentials(GROUPS[g], NGR * l + g + NGR0 + 1)

            with act.Fori(0, L - 1) as l:
                experts(l)
                exponentials(GROUPS[NGR - 1], NGR * l + NGR + NGR0)
            experts(L - 1, final=True)
            for b in range(B):
                sl = slice(TPB * b, TPB * b + TPB)
                act.wait_ge(got_loaded[b], 16)
                nc.scalar.activation(std[:, sl], got[:, sl, D + 1], ACT.Sqrt, bias=eps[:, 0:1]).then_inc(fin_std, 1)
            for b in range(1, B, 2):
                act.wait_ge(fin_shift, b // 2 + 1)
                for t in range(TPB * b, TPB * b + TPB):
                    last = nc.scalar.activation(got[:, t, 0:D], got[:, t, 0:D], ACT.Identity,
                                                bias=shift[:, t:t + 1], scale=rstd[:, t:t + 1])
                last.then_inc(fin_norm[1], 1)

        @block.vector
        def _(dve):
            def variance(k, rows_of, tiles):
                for t in tiles:
                    last = nc.vector.bn_stats(stats[:, t, :], rows_of(t))
                last.then_inc(ln_stat, 1)
                dve.wait_ge(ln_stat, B + k)
                for t in tiles:
                    last = nc.vector.bn_aggr(meanvar[:, t, :], stats[:, t, :])
                last.then_inc(ln_var, 1)

            def inverse(k, tiles):
                dve.wait_ge(ln_std, k + 1)
                sl = slice(tiles[0], tiles[-1] + 1)
                nc.vector.reciprocal(rstd[:, sl], std[:, sl]).then_inc(ln_rstd, 1)
                dve.wait_ge(ln_rstd, k + 1)

            def aggregate(b):
                dve.wait_ge(ln_stat, b + 1)
                for t in range(TPB * b, TPB * b + TPB):
                    last = nc.vector.bn_aggr(meanvar[:, t, :], stats[:, t, :])
                return last

            for b in range(B):
                dve.wait_ge(x_loaded[b], 16)
                for t in range(TPB * b, TPB * b + TPB):
                    last = nc.vector.bn_stats(stats[:, t, :], x_sb[:, t, :])
                last.then_inc(ln_stat, 1)
                if b > 0:
                    aggregate(b - 1)
            aggregate(B - 1).then_inc(ln_var, 1)
            dve.wait_ge(prep_T, 1)
            nc.vector.tensor_scalar(bcol[:, :], ps_v[:, 0:2 * NPAIR], W_SCALE, None, ALU.mult).then_inc(prep_done, 1)
            inverse(0, range(NT))
            late = slice(TPB * NV, NT)
            nc.vector.scalar_tensor_tensor(out=shift[:, late], in0=meanvar[:, late, 0], scalar=-1.0, in1=rstd[:, late],
                                           op0=ALU.mult, op1=ALU.mult).then_inc(shift_ready, 1)
            for b in range(NV):
                for t in range(TPB * b, TPB * b + TPB):
                    last = nc.vector.tensor_scalar(xn[:, t, 0:D], x_sb[:, t, :], meanvar[:, t, 0:1],
                                                   rstd[:, t:t + 1], ALU.subtract, ALU.mult)
                last.then_inc(ln_out, 1)
            for n, (kind, m, g) in enumerate(PREP[:NPREP]):
                dve.wait_ge(prep_hi, n + 1)
                if kind == "w":
                    nc.vector.scalar_tensor_tensor(out=wT_lo[:, m, 512 * g:512 * g + 512], in0=ps[n % 4][:, :],
                                                   scalar=W_SCALE, in1=wT_hi[:, m, 512 * g:512 * g + 512],
                                                   op0=ALU.mult, op1=ALU.subtract).then_inc(prep_done, 1)
                else:
                    nc.vector.tensor_tensor(xT_lo[:, S * m:S * m + S], ps[n % 4][:, :], xT_hi[:, S * m:S * m + S],
                                            ALU.subtract).then_inc(prep_done, 1)

            def low(dst, u, src_, hi, done, col, i):
                dve.wait_ge(hi, i + 1)
                nc.vector.scalar_tensor_tensor(out=dst[:, u, 1, :], in0=src_[:, :], scalar=bcol[:, bass.ds(col, 1)],
                                               in1=dst[:, u, 0, :], op0=ALU.add, op1=ALU.subtract).then_inc(done, 1)

            def values(i, u, pair):
                dve.wait_ge(v_ready, i + 1)
                nc.vector.scalar_tensor_tensor(
                    out=v_sb[:, u, :, :], in0=ps_v[:, :].rearrange("p (t c) -> p t c", t=TPB), scalar=1.0 / W_SCALE,
                    in1=vb_all[:, bass.ds(pair * P, P)].unsqueeze(1).broadcast_to([P, TPB, P]),
                    op0=ALU.mult, op1=ALU.add).then_inc(v_out, 1)

            def scale_values(i, u, kt):
                dve.wait_ge(exp_done, 8 * i + (2 * kt + 2))
                nc.vector.reciprocal(rsum[:, kt, :], esum[:, kt, :]).then_inc(rsum_done, 1)
                dve.wait_ge(rsum_done, 4 * i + (kt + 1))
                nc.vector.tensor_tensor(vp[:, kt, :].rearrange("p (h c) -> p h c", h=2),
                                        v_sb[:, u, kt, :].rearrange("p (h c) -> p h c", h=2),
                                        rsum[:, kt, :].unsqueeze(2).broadcast_to([P, 2, DH]),
                                        ALU.mult).then_inc(vp_done, 1)

            def pair_step(i, u, ahead=2, first=False):
                for kt in range(TPB):
                    for hd in range(2):
                        dve.wait_ge(scores_ready, 8 * i + (2 * kt + hd + 1))
                        nc.vector.tensor_reduce(mx[:, kt, hd:hd + 1], ps[(2 * kt + hd) % 4][:, :], AX_X,
                                                ALU.max).then_inc(max_done, 1)
                    if kt >= 1:
                        scale_values(i, u, kt - 1)
                    elif not first:
                        scale_values(i - 1, 1 - u, TPB - 1)
                    if kt == 0 and not first:
                        values(i, u, i % NPAIR)
                    if ahead >= 2 and kt == 2:
                        low(k_pair, u, ps_k, k_hi, k_lo, (i + 2) % NPAIR + NPAIR, i + 2)
                    if ahead >= 2 and kt == 3:
                        low(q_pair, u, ps_q, q_hi, q_lo, (i + 2) % NPAIR, i + 2)

            low(k_pair, 0, ps_k, k_hi, k_lo, NPAIR, 0)
            low(q_pair, 0, ps_q, q_hi, q_lo, 0, 0)
            dve.wait_ge(vb_loaded, 16)
            values(0, 0, 0)
            low(k_pair, 1, ps_k, k_hi, k_lo, NPAIR + 1, 1)
            low(q_pair, 1, ps_q, q_hi, q_lo, 1, 1)
            dve.wait_ge(consts, 12)
            nc.vector.tensor_copy(ones_row[:, :], one_row[0:1, 0:1].broadcast_to([1, P]))
            dve.wait_ge(lb_hi, 1)
            nc.vector.tensor_tensor(lb_parts[:, 1, :], lb_row[:, :], lb_parts[:, 0, :], ALU.subtract)
            for n in range(NPREP, len(PREP)):
                _, m, g = PREP[n]
                dve.wait_ge(prep_T, n + 2)
                nc.vector.tensor_copy(lwT[:, 4 * g:4 * g + 4, :].rearrange("p a b -> p (a b)"),
                                      ps[n % 4][:, :]).then_inc(prep_done, 1)
            pair_step(0, 0, first=True)
            pair_step(1, 1)
            with dve.Fori(1, NP // 2 - 1) as g:
                for u in range(2):
                    pair_step(2 * g + u, u)
            pair_step(NP - 2, 0, ahead=1)
            pair_step(NP - 1, 1, ahead=0)
            scale_values(NP - 1, 1, TPB - 1)

            for b in range(B):
                tiles = range(TPB * b, TPB * b + TPB)
                k = 1 + 2 * b
                dve.wait_ge(proj_ready, b + 1)
                variance(k, lambda t: ps_out[b][:, (t % TPB) * P:(t % TPB + 1) * P], tiles)
                inverse(k, tiles)
                sl = slice(TPB * b, TPB * b + TPB)
                nc.vector.scalar_tensor_tensor(out=shift[:, sl], in0=meanvar[:, sl, 0], scalar=-1.0, in1=rstd[:, sl],
                                               op0=ALU.mult, op1=ALU.mult).then_inc(shift_ready, 1)
                dve.wait_ge(att_done, b + 1)
                dve.wait_ge(x_loaded[b], 32)
                nc.vector.tensor_tensor(x_sb[:, sl, :], x_sb[:, sl, :], att_n[:, sl, 0:D], ALU.add).then_inc(x1_done, 1)
                dve.wait_ge(x1_done, b + 1)
                variance(k + 1, lambda t: x_sb[:, t, :], tiles)
                inverse(k + 1, tiles)
                for t in tiles:
                    last = nc.vector.tensor_scalar(xn[:, t, 0:D], x_sb[:, t, :], meanvar[:, t, 0:1],
                                                   rstd[:, t:t + 1], ALU.subtract, ALU.mult)
                last.then_inc(ln_out, 1)

            count = [0]

            def step(ins, base):
                count[0] += 1
                ins.then_inc(route, 1)
                dve.wait_ge(route, base + count[0])

            def pair(one, other, base):
                one.then_inc(route, 1)
                count[0] += 1
                step(other, base)

            V = nc.vector

            def best(n, sl, base, lgs, rels, all_real=False):
                w = sl.stop - sl.start
                if n == 0:
                    dve.wait_ge(lg_copied, lgs)
                    step(V.tensor_reduce(lmax[:, sl], lg[:, sl, :], AX_X, ALU.max), base)
                    V.tensor_tensor(rel[:, sl, :], lg[:, sl, :], lmax[:, sl].unsqueeze(2).broadcast_to([P, w, E]),
                                    ALU.subtract).then_inc(rel_ready, 1)
                    dve.wait_ge(rel_ready, rels)
                elif n == 1:
                    step(V.scalar_tensor_tensor(out=cand[:, sl, :], in0=rel[:, sl, :], scalar=0.0, in1=expert_m[:, sl, :],
                                                op0=ALU.is_equal, op1=ALU.mult), base)
                elif n == 2:
                    step(V.tensor_reduce(expert[:, sl], cand[:, sl, :], AX_X, ALU.min), base)
                    if not all_real:
                        step(V.tensor_tensor(expert[:, sl], expert[:, sl], empty[:, sl], ALU.add), base)
                elif n == 3:
                    V.tensor_tensor(chosen[:, sl, :], expert_m[:, sl, :], expert[:, sl].unsqueeze(2).broadcast_to([P, w, E]),
                                    ALU.is_equal).then_inc(chosen_ready, 1)

            def weights(sl, base, rels, rows_):
                dve.wait_ge(exp_ready, rels)
                step(V.tensor_reduce(zsum[:, sl], ex[:, sl, :], AX_X, ALU.add), base)
                step(V.reciprocal(weight[:, sl], zsum[:, sl]), base)
                V.tensor_scalar(rows_[:, sl, D + 1], weight[:, sl], 0.5, None, ALU.mult).then_inc(weight_ready, 1)

            def places(n, sl, base, reads, counts, all_real=False):
                if n == 0:
                    dve.wait_ge(ranks_ready, counts)
                    V.tensor_tensor(ranked[:, sl, :], ps_rank[:, sl.start * E:sl.stop * E].rearrange("p (j e) -> p j e", e=E),
                                    chosen[:, sl, :], ALU.mult).then_inc(ranks_read, 1)
                    dve.wait_ge(ranks_read, reads)
                    step(V.tensor_reduce(rank[:, sl], ranked[:, sl, :], AX_X, ALU.add), base)
                elif n == 1:
                    step(V.tensor_scalar(tile_in[:, sl], rank[:, sl], -(P - 1) / 2.0, 1.0 / P, ALU.add, ALU.mult), base)
                    step(V.tensor_scalar(tile_in[:, sl], tile_in[:, sl], ROUND, ROUND, ALU.add, ALU.subtract), base)
                    step(V.scalar_tensor_tensor(out=pos_b[:, sl], in0=tile_in[:, sl], scalar=-float(P), in1=rank[:, sl],
                                                op0=ALU.mult, op1=ALU.add), base)
                    if not all_real:
                        step(V.tensor_tensor(tile_in[:, sl], tile_in[:, sl], empty[:, sl], ALU.add), base)
                elif n == 2:
                    step(one_hots(sl), base)

            def one_hots(sl):
                for j in range(sl.start, sl.stop):
                    last = V.tensor_scalar(on_b[:, j, :], iota_b[:, :], pos_b[:, j:j + 1], label[:, j:j + 1],
                                           ALU.is_equal, ALU.mult)
                return last

            def finish(sl, base, counts, l, all_real=False):
                n = sl.stop
                dve.wait_ge(ranks_ready, counts)
                pair(V.tensor_tensor(ranked[:, sl, :], ps_rank[:, sl.start * E:sl.stop * E].rearrange("p (j e) -> p j e", e=E),
                                     chosen[:, sl, :], ALU.mult),
                     V.tensor_scalar(tiles_e[:, :], ps_rank[:, NS * E:], (P - 1) / 2.0, 1.0 / P, ALU.add, ALU.mult), base)
                pair(V.tensor_reduce(rank[:, sl], ranked[:, sl, :], AX_X, ALU.add),
                     V.tensor_scalar(tiles_e[:, :], tiles_e[:, :], ROUND, ROUND, ALU.add, ALU.subtract), base)
                pair(V.tensor_scalar(tile_in[:, sl], rank[:, sl], -(P - 1) / 2.0, 1.0 / P, ALU.add, ALU.mult),
                     V.tensor_tensor_scan(cum_e[:, :], one_row[:, :], tiles_e[:, :], 0.0, ALU.mult, ALU.add), base)
                pair(V.tensor_scalar(tile_in[:, sl], tile_in[:, sl], ROUND, ROUND, ALU.add, ALU.subtract),
                     V.tensor_tensor(first_e[:, :], cum_e[:, :], tiles_e[:, :], ALU.subtract), base)
                pair(V.scalar_tensor_tensor(out=pos_b[:, sl], in0=tile_in[:, sl], scalar=-float(P), in1=rank[:, sl],
                                            op0=ALU.mult, op1=ALU.add),
                     V.tensor_tensor(first[:, 0:n, :], chosen[:, 0:n, :], first_e[:, :].unsqueeze(1).broadcast_to([P, n, E]),
                                     ALU.mult), base)
                if all_real:
                    step(V.tensor_reduce(pos_a[:, 0:n], first[:, 0:n, :], AX_X, ALU.add), base)
                else:
                    pair(V.tensor_tensor(tile_in[:, sl], tile_in[:, sl], empty[:, sl], ALU.add),
                         V.tensor_reduce(pos_a[:, 0:n], first[:, 0:n, :], AX_X, ALU.add), base)
                step(V.tensor_tensor(pos_a[:, 0:n], pos_a[:, 0:n], tile_in[:, 0:n], ALU.add), base)
                for lo, hi in ((0, n // 2), (n // 2, n)):
                    V.tensor_tensor(on_a[:, lo:hi, :], iota_a[:, :].unsqueeze(1).broadcast_to([P, hi - lo, NS]),
                                    pos_a[:, lo:hi].unsqueeze(2).broadcast_to([P, hi - lo, NS]),
                                    ALU.is_equal).then_inc(on_a_ready, 1)
                one_hots(sl).then_inc(on_b_ready, 1)
                dve.wait_ge(inv_ready, l + 1)
                step(V.tensor_scalar(beyond[:, :], ps_inv[:, 0:NS], 0.0, 2.0 * HALF, ALU.is_lt, ALU.mult), base)
                V.tensor_tensor(src_i[:, :], ps_inv[:, 0:NS], beyond[:, :], ALU.add).then_inc(src_ready, 1)
                step(V.tensor_scalar(empty[:, :], ps_inv[:, 0:NS], 0.0, INVALID, ALU.is_equal, ALU.mult), base)
                step(V.tensor_tensor(under[:, :, :], cum_e[:, :].unsqueeze(1).broadcast_to([P, NS, E]),
                                     iota_a[:, :].unsqueeze(2).broadcast_to([P, NS, E]), ALU.is_le), base)
                step(V.tensor_reduce(eid[:, :], under[:, :, :], AX_X, ALU.add), base)
                V.tensor_scalar(w_off[:, :], eid[:, :], float(E - 1), float(FF), ALU.min, ALU.mult).then_inc(w_off_ready, 1)

            def experts(l, final=False):
                base = l * NS
                low_part(base, 0)
                for s in range(NS + (3 if final else 4)):
                    t = s + 1
                    if t < NS:
                        low_part(base, t)
                    t = s
                    if t < NS:
                        dve.wait_ge(th_done, base + (t + 1))
                        if t >= 2:
                            dve.wait_ge(hT_in, base + (t - 1))
                        V.scalar_tensor_tensor(out=act_h[:, t % 2, :], in0=th[:, t % 2, :], scalar=1.0,
                                               in1=ps_h[t % 2][:, :], op0=ALU.add, op1=ALU.mult).then_inc(h_done, 1)
                    if final:
                        t = s - 3
                        if t >= 0:
                            dve.wait_ge(y_done, base + t + 1)
                            V.scalar_tensor_tensor(out=tok_i[:, t:t + 1], in0=empty[:, t:t + 1], scalar=1000.0,
                                                   in1=xg[:, t, D:D + 1], op0=ALU.mult, op1=ALU.add)
                            V.bn_stats(slot_stats[:, t % 2, :], xg[:, t, 0:D]).then_inc(slot_stat, 1)
                            dve.wait_ge(slot_stat, t + 1)
                            V.bn_aggr(xg[:, t, D:D + 2], slot_stats[:, t % 2, :]).then_inc(slot_done, 1)
                        continue
                    for g in range(NGR - 1):
                        for n in range(8):
                            if s == ROUTE_AT[g][n]:
                                route_step(l, g, n)

            def carry(sl, base, start):
                step(V.tensor_reduce(part[:, :], chosen[:, sl, :].rearrange("p j e -> p e j"), AX_X, ALU.add), base)
                step(V.tensor_copy(earlier[:, :], part[:, :]) if start else
                     V.tensor_tensor(earlier[:, :], earlier[:, :], part[:, :], ALU.add), base)

            def low_part(base, t):
                dve.wait_ge(xT_out, base + (t + 1))
                if t >= 2:
                    dve.wait_ge(h_in, base + (t - 1))
                V.tensor_tensor(slot_lo[:, t % 2, :], ps_xT[:, 0:P], slot_hi[:, t % 2, :], ALU.subtract).then_inc(lo_out, 1)

            def route_step(l, g, n):
                sl = slice(GROUPS[g][0], GROUPS[g][-1] + 1)
                base = ROUTE0_STEPS + ROUTE_STEPS * l
                c = NGR * l + g + NGR0 + 1
                if n < 4:
                    best(n, sl, base, NS * l + GROUPS[g][-1] + NGR0 + 1, c)
                elif n == 4:
                    weights(sl, base, c, xg)
                else:
                    places(n - 5, sl, base, (NGR - 1) * l + g + NGR0, c)
                    if n == 5:
                        carry(sl, base, g == 0)

            dve.wait_ge(filled, 1)
            dve.wait_ge(consts, 12)
            dve.wait_ge(numbered, 1)
            for g, tiles in enumerate(GROUPS0):
                sl = slice(tiles[0], tiles[-1] + 1)
                for n in range(4):
                    best(n, sl, 0, g + 1, g + 1, all_real=True)
                if g < NGR0 - 1:
                    for n in range(2):
                        places(n, sl, 0, g + 1, g + 1, all_real=True)
                        if n == 0:
                            carry(sl, 0, g == 0)
            places(2, slice(0, GROUPS0[-1][0]), 0, 0, 0)
            for g, tiles in enumerate(GROUPS0):
                weights(slice(tiles[0], tiles[-1] + 1), 0, g + 1, xn)
            finish(sl, 0, NGR0, 0, all_real=True)
            assert count[0] == ROUTE0_STEPS, count[0]
            for e in range(E - DVE_SPLITS, E):
                dve.wait_ge(w1_hi_ready, e + 1)
                V.tensor_tensor(w1_lo[:, e * FF:(e + 1) * FF], w1_raw[:, e * FF:(e + 1) * FF], w1_hi[:, e * FF:(e + 1) * FF],
                                ALU.subtract).then_inc(w1_lo_dve, 1)
            with dve.Fori(0, L - 1) as l:
                count[0] = 0
                experts(l)
                for n in range(5):
                    route_step(l, NGR - 1, n)
                finish(slice(GROUPS[-1][0], NS), ROUTE0_STEPS + ROUTE_STEPS * l, NGR * l + NGR + NGR0, l + 1)
                assert count[0] == ROUTE_STEPS, count[0]
            experts(L - 1, final=True)

            order = [0, 1, 3, 2]

            def fin_inverse(b):
                sl = slice(TPB * b, TPB * b + TPB)
                dve.wait_ge(fin_std, b + 1)
                V.reciprocal(rstd[:, sl], std[:, sl]).then_inc(fin_rstd, 1)
                dve.wait_ge(fin_rstd, order.index(b) + 1)
                if b % 2:
                    V.scalar_tensor_tensor(out=shift[:, sl], in0=got[:, sl, D], scalar=-1.0, in1=rstd[:, sl],
                                           op0=ALU.mult, op1=ALU.mult).then_inc(fin_shift, 1)

            def fin_normalise(b):
                for t in range(TPB * b, TPB * b + TPB):
                    last = V.tensor_scalar(got[:, t, 0:D], got[:, t, 0:D], got[:, t, D:D + 1], rstd[:, t:t + 1],
                                           ALU.subtract, ALU.mult)
                last.then_inc(fin_norm[0], 1)

            def fin_add(b):
                sl = slice(TPB * b, TPB * b + TPB)
                dve.wait_ge(fin_norm[b % 2], b // 2 + 1)
                V.tensor_tensor(got[:, sl, 0:D], got[:, sl, 0:D], x_sb[:, sl, :], ALU.add).then_inc(fin_ready, 1)

            fin_inverse(0)
            fin_inverse(1)
            fin_normalise(0)
            fin_add(0)
            fin_inverse(3)
            fin_inverse(2)
            fin_normalise(2)
            for b in range(1, B):
                fin_add(b)


_INS = ["L0_attn_x", "L0_attn_q_w", "L0_attn_q_b", "L0_attn_k_w", "L0_attn_k_b", "L0_attn_v_w", "L0_attn_v_b",
        "L0_attn_l_w", "L0_attn_l_b", "L0_ffn_routers", "L0_ffn_W1", "L0_ffn_W2"]


def kernel(**inputs):
    import numpy as np
    import concourse.bacc as bacc
    from concourse.bass_utils import run_bass_kernel_spmd

    nc = bacc.Bacc("TRN2", target_bir_lowering=False, num_devices=1)
    arrays, args = {}, []
    for name in _INS:
        a = np.ascontiguousarray(inputs[name])
        arrays[f"in_{name}"] = a
        args.append(nc.dram_tensor(f"in_{name}", a.shape, mybir.dt.from_np(a.dtype), kind="ExternalInput").ap())
    x = arrays["in_L0_attn_x"]
    args.append(nc.dram_tensor("out", x.shape, F32, kind="ExternalOutput").ap())
    sandwich_kernel(nc, *args)
    r = run_bass_kernel_spmd(nc, [arrays], core_ids=[0])
    return r.results[0]["out"]
```
